# Optimizing a Trainium2 kernel written in Bass

```python
import numpy as np
import jax
import jax.numpy as jnp

def _softmax(x, axis=-1):
    return jax.nn.softmax(x, axis=axis)

def _gelu(x):
    return jax.nn.gelu(x, approximate=True)

def _silu(x):
    return jax.nn.silu(x)

def _sigmoid(x):
    return jax.nn.sigmoid(x)

def _layernorm(x, axis=-1, eps=1e-05):
    m = jnp.mean(x, axis=axis, keepdims=True)
    v = jnp.var(x, axis=axis, keepdims=True)
    return (x - m) / jnp.sqrt(v + eps)

def _scatter_add(tgt, idx, src, axis=0):
    return tgt.at[idx].add(src)

def _segment_sum(src, seg, n):
    return jax.ops.segment_sum(src, seg, n)
kernel_name = 'mk_xattn_ffn_d1_seqx_r4_a16060'

def setup_inputs(seed: int=0):
    np.random.seed(seed)
    _w = jnp.asarray

    def _rec_inputs():
        import jax
        import jax.numpy as jnp
        _rk = jax.random.key(seed)
        x = 7.22e-05 + 1 * jax.random.normal(jax.random.fold_in(_rk, 1), (4, 512, 512), jnp.float32)
        _lenS = 512 - jax.random.randint(jax.random.fold_in(_rk, 7), (4,), 0, max(1, 512 // 4) + 1, jnp.int32)
        _lenS2 = 512 - jax.random.randint(jax.random.fold_in(_rk, 8), (4,), 0, max(1, 512 // 4) + 1, jnp.int32)
        _ctx_2048P = jax.random.normal(jax.random.fold_in(_rk, 11), (4, 16, 512), jnp.float32)
        _ctx_2048c = jax.random.dirichlet(jax.random.fold_in(_rk, 511), 0.3 * jnp.ones((16,), jnp.float32), (4, 512))
        _ctx_2048t = jnp.einsum('bsk,bkd->bsd', _ctx_2048c, _ctx_2048P)
        _ctx_2048t = _ctx_2048t * jax.lax.rsqrt(jnp.mean(jnp.square(_ctx_2048t)) + 1e-12) * 0.953939
        ctx_2048 = 4.13588e-05 + 0.999923 * (_ctx_2048t + 0.3 * jax.random.normal(jax.random.fold_in(_rk, 611), (4, 512, 512), jnp.float32))
        return (x, ctx_2048)
    x, ctx_2048 = _rec_inputs()

    def _L0_xattn_setup():
        import jax, jax.numpy as jnp
        import numpy as np
        N_HEAD = 8
        key = jax.random.key(seed)
        k1, k2, k3 = jax.random.split(key, 3)
        B, D, L = (4, 256, 512)
        q = jax.random.normal(k1, (B, D, L), dtype=jnp.float32)
        k = jax.random.normal(k2, (B, D, L), dtype=jnp.float32)
        v = jax.random.normal(k3, (B, D, L), dtype=jnp.float32)
        gamma = jnp.ones((), dtype=jnp.float32)
        return {'q': q, 'k': k, 'v': v, 'gamma': gamma}
    _L0_xattn_all = _L0_xattn_setup()
    _L0_xattn_in = {k: v for k, v in _L0_xattn_all.items() if k in ('gamma',)}
    del _L0_xattn_all

    def _L0_ffn_setup():
        import jax, jax.numpy as jnp
        import numpy as np
        E = 8
        TOP_K = 2
        H = 512
        I = 352
        SI = 1408
        key = jax.random.key(seed)
        ks = jax.random.split(key, 9)
        s = lambda fan_in: 1.0 / np.sqrt(fan_in)
        return {'hidden_states': jax.random.normal(ks[0], (4, 512, H), dtype=jnp.float32), 'router_w': jax.random.normal(ks[1], (E, H), dtype=jnp.float32) * s(H), 'w_gate': jax.random.normal(ks[2], (E, H, I), dtype=jnp.float32) * s(H), 'w_up': jax.random.normal(ks[3], (E, H, I), dtype=jnp.float32) * s(H), 'w_down': jax.random.normal(ks[4], (E, I, H), dtype=jnp.float32) * s(I), 'sw_gate': jax.random.normal(ks[5], (H, SI), dtype=jnp.float32) * s(H), 'sw_up': jax.random.normal(ks[6], (H, SI), dtype=jnp.float32) * s(H), 'sw_down': jax.random.normal(ks[7], (SI, H), dtype=jnp.float32) * s(SI), 'shared_gate_w': jax.random.normal(ks[8], (H,), dtype=jnp.float32) * s(H)}
    _L0_ffn_all = _L0_ffn_setup()
    _L0_ffn_in = {k: v for k, v in _L0_ffn_all.items() if k in ('router_w', 'w_gate', 'w_up', 'w_down', 'sw_gate', 'sw_up', 'sw_down', 'shared_gate_w')}
    del _L0_ffn_all
    return {'x': x, 'ctx_2048': ctx_2048, 'L0_xattn_gamma': _L0_xattn_in['gamma'], 'L0_ffn_router_w': _L0_ffn_in['router_w'], 'L0_ffn_w_gate': _L0_ffn_in['w_gate'], 'L0_ffn_w_up': _L0_ffn_in['w_up'], 'L0_ffn_w_down': _L0_ffn_in['w_down'], 'L0_ffn_sw_gate': _L0_ffn_in['sw_gate'], 'L0_ffn_sw_up': _L0_ffn_in['sw_up'], 'L0_ffn_sw_down': _L0_ffn_in['sw_down'], 'L0_ffn_shared_gate_w': _L0_ffn_in['shared_gate_w']}

def reference(x, ctx_2048, L0_xattn_gamma, L0_ffn_router_w, L0_ffn_w_gate, L0_ffn_w_up, L0_ffn_w_down, L0_ffn_sw_gate, L0_ffn_sw_up, L0_ffn_sw_down, L0_ffn_shared_gate_w):
    import jax
    import jax.numpy as jnp

    def _L0_xattn_ref(q, k, v, gamma):
        import jax, jax.numpy as jnp
        import numpy as np
        N_HEAD = 8
        B, Dq, Lq = q.shape
        Dv, Lk = (v.shape[-2], v.shape[-1])
        h = N_HEAD
        dq = Dq // h
        dv = Dv // h
        qh = q.reshape(B, h, dq, Lq)
        kh = k.reshape(B, h, dq, Lk)
        vh = v.reshape(B, h, dv, Lk)
        scale = 1.0 / jnp.sqrt(jnp.asarray(dq, dtype=q.dtype))
        qk = jnp.einsum('bhdq,bhdl->bhql', qh, kh) * scale
        sm = jax.nn.softmax(qk, axis=-1)
        ret = jnp.einsum('bhql,bhdl->bhdq', sm, vh)
        ret = ret.reshape(B, Dv, Lq)
        return gamma * ret

    def _L0_ffn_ref(hidden_states, router_w, w_gate, w_up, w_down, sw_gate, sw_up, sw_down, shared_gate_w):
        import jax, jax.numpy as jnp
        import numpy as np
        E = 8
        TOP_K = 2
        H = 512
        I = 352
        SI = 1408
        B, S, Hd = hidden_states.shape
        x = hidden_states.reshape(-1, Hd)
        shared = jnp.einsum('ts,sh->th', jax.nn.silu(x @ sw_gate) * (x @ sw_up), sw_down)
        logits = x @ router_w.T
        probs = jax.nn.softmax(logits.astype(jnp.float32), axis=-1)
        top_w, top_i = jax.lax.top_k(probs, TOP_K)
        top_w = top_w / jnp.sum(top_w, axis=-1, keepdims=True)
        combine = jnp.sum(jax.nn.one_hot(top_i, E, dtype=x.dtype) * top_w[..., None].astype(x.dtype), axis=1)
        h = jax.nn.silu(jnp.einsum('th,ehi->eti', x, w_gate)) * jnp.einsum('th,ehi->eti', x, w_up)
        expert_out = jnp.einsum('eti,eih->eth', h, w_down)
        routed = jnp.einsum('eth,te->th', expert_out, combine)
        shared_out = jax.nn.sigmoid(x @ shared_gate_w)[:, None] * shared
        return (routed + shared_out).reshape(B, S, Hd)
    x = x + _L0_xattn_ref(_layernorm(x, axis=-1), ctx_2048, ctx_2048, L0_xattn_gamma)
    x = x + _L0_ffn_ref(_layernorm(x, axis=-1), L0_ffn_router_w, L0_ffn_w_gate, L0_ffn_w_up, L0_ffn_w_down, L0_ffn_sw_gate, L0_ffn_sw_up, L0_ffn_sw_down, L0_ffn_shared_gate_w)
    return x

_drawn_inputs = setup_inputs


def setup_inputs(seed=0):
    import zlib

    import numpy as np

    out = dict(_drawn_inputs(seed))
    spreads = {}
    factors = {}
    for name, (base, spread) in spreads.items():
        noise = np.random.default_rng([zlib.crc32(name.encode()), seed]).standard_normal(out[name].shape)
        drawn = base * np.exp(spread * noise) if base else spread * noise
        out[name] = jnp.asarray(drawn.astype(out[name].dtype))
    for name, factor in factors.items():
        out[name] = (out[name] * factor).astype(out[name].dtype)
    return out
```

```python
from contextlib import ExitStack

import concourse.bass as bass
from concourse import mybir

ALU = mybir.AluOpType
ACT = mybir.ActivationFunctionType
AX_X = mybir.AxisListType.X
F32 = mybir.dt.float32
F32R = mybir.dt.float32r
I32 = mybir.dt.int32
U32 = mybir.dt.uint32

P = 128
EPS = 1e-5


def xattn_moe_kernel(nc, x, ctx_in, gamma, router_w, w_gate, w_up, w_down, sw_gate, sw_up, sw_down, shared_gate_w, out):
    B, D, L = x.shape
    NH = 8
    DH = D // NH
    T = B * D
    H = L
    E, _, I = w_gate.shape
    SI = sw_gate.shape[1]
    NT = T // P
    HC = H // P
    LC = L // P
    QC = L // P
    NB = T // 512
    TB = 512 // P
    SC = SI // P
    IC = (I + P - 1) // P
    IR = I - (IC - 1) * P
    TOPK = 2
    SLOTS = (TOPK * T + (P - 1) * E) // P
    NR = E + 1
    NI = NT // 2
    assert DH == 64 and D == 512 and L == 512 and SI % P == 0 and NT % 2 == 0 and SLOTS == 39

    x_t = x.rearrange("b d l -> (b d) l").rearrange("(t p) l -> t p l", p=P)
    c_t = ctx_in.rearrange("b d l -> (b d) l").rearrange("(t p) l -> t p l", p=P)
    c_h = ctx_in.rearrange("b d l -> (b d) l").rearrange("(t s p) l -> t p s l", s=2, p=DH)
    x2_d = nc.dram_tensor("x2_rows", (T, H), F32, kind="Internal").ap()
    x2_t = x2_d.rearrange("(t p) h -> t p h", p=P)
    xn_d = nc.dram_tensor("x2_normed_rows", (T + P, H), F32, kind="Internal").ap()
    xT_d = nc.dram_tensor("x2_normed_transposed", (NT, P, H), F32, kind="Internal").ap()
    meta_d = nc.dram_tensor("slot_rows", (SLOTS * P, 2), I32, kind="Internal").ap()

    ctx = ExitStack()
    with ctx:
        def sem(name):
            return ctx.enter_context(nc.semaphore(name))

        def sems(name, n):
            return [sem(f"{name}{j}") for j in range(n)]

        base = (nc.sbuf_base + 31) // 32 * 32
        cursor = [base]

        def place(name, shape, dt=F32):
            n = 4
            for d in shape[1:]:
                n *= d
            t = nc.alloc_sbuf_tensor_at(name, list(shape), dt, offset=cursor[0])
            cursor[0] += (n + 31) // 32 * 32
            assert cursor[0] <= nc.sbuf_usable_end, (name, cursor[0])
            return t

        ident = place("ident", [P, P])
        tri = place("tri", [P, P])
        ones = place("ones", [P, P])
        rgT = place("rgT", [P, HC, NR])
        gam = place("gam", [P, 1])
        mhalf = place("mhalf", [P, 1])
        lg_all = place("lg_all", [P, NT, NR])
        sig = place("sig", [P, NT])
        posi = place("posi", [P, NT, TOPK], I32)
        msrc = place("msrc", [P, NT, TOPK, 2], I32)
        slot_tab = place("slot_tab", [1, 40], I32)
        mini = place("mini", [P, SLOTS, 2], I32)
        stats = place("stats", [P, 2, 6])
        aggr = place("aggr", [P, 2, 2])
        vare = place("vare", [P, 2, 1])
        rstd = place("rstd", [P, 2, 1])
        negmax = place("negmax", [P, 2, QC])
        rsum = place("rsum", [P, 2, QC])
        rinv = place("rinv", [P, 2, QC])
        mt = [place(f"mt{j}", [P, 2], I32) for j in range(4)]
        fixed_end = cursor[0]

        WCH = 3 * 512
        EW = 2 * HC * I + IC * H
        big = cursor[0]
        xb = [place(f"xb{j}", [P, L]) for j in range(2)]
        x2b = [place(f"x2b{j}", [P, L]) for j in range(2)]
        cn = [place(f"cn{j}", [P, L]) for j in range(2)]
        cd = [place(f"cd{j}", [P, 2, L]) for j in range(2)]
        kh = [place(f"kh{j}", [P, 2, L], F32R) for j in range(2)]
        kl = [place(f"kl{j}", [P, 2, L], F32R) for j in range(2)]
        xn = [place(f"xn{j}", [P, L]) for j in range(2)]
        qs = [place(f"qs{j}", [P, L], F32R) for j in range(2)]
        vs = [place(f"vs{j}", [P, LC, 2, 2, DH], F32R) for j in range(2)]
        pb = [place(f"pb{j}", [P, QC, L]) for j in range(2)]
        pth = [place(f"pth{j}", [P, L], F32R) for j in range(4)]
        ptl = [place(f"ptl{j}", [P, L], F32R) for j in range(4)]
        x2n = [place(f"x2n{j}", [P, H]) for j in range(2)]
        x2T = [place(f"x2T{j}", [P, HC, P]) for j in range(2)]
        rg = place("rg", [NR, H])
        zrow = place("zrow", [P, H])
        stage1_end = cursor[0]
        cursor[0] = big
        wsp = [place(f"wsp{c}", [P, 2, WCH], F32R) for c in range(SC)]
        cursor[0] = big
        wex = place("wex", [P, E, EW])
        big_end = cursor[0]
        assert stage1_end <= big_end
        stg0 = cursor[0]
        stg = [place(f"stg{j}", [P, 3, 512]) for j in range(2)]
        stg_end = cursor[0]
        xhl0 = cursor[0]
        xh = place("xh", [P, 2, TB, HC, P], F32R)
        xl = place("xl", [P, 2, TB, HC, P], F32R)
        sg = [place(f"sg{j}", [P, 512]) for j in range(2)]
        hh = [place(f"hh{j}", [P, 512], F32R) for j in range(2)]
        hl = [place(f"hl{j}", [P, 512], F32R) for j in range(2)]
        xr = [place(f"xr{j}", [P, H]) for j in range(2)]
        tables0 = cursor[0]
        cursor[0] = stg0
        xg = [place(f"xg{j}", [P, H]) for j in range(4)]
        ls = place("ls", [P, NT, E])
        pre_s = place("pre_s", [P, NT, E])
        tot_s = place("tot_s", [P, NT, E])
        carry = place("carry", [P, NT, E])
        m1 = place("m1", [P, NT, E])
        m2 = place("m2", [P, NT, E])
        assert cursor[0] <= stg_end
        cursor[0] = xhl0
        xT3 = [place(f"xT3{j}", [P, HC, P]) for j in range(2)]
        h3 = [place(f"h3{j}", [P, I]) for j in range(2)]
        hT3 = [place(f"hT3{j}", [P, IC, P]) for j in range(2)]
        y3 = [place(f"y3{j}", [P, H]) for j in range(2)]
        assert cursor[0] <= xhl0 + 4 * 2048 * 2
        cursor[0] = tables0
        tv = place("tv", [P, NT, 8])
        ti = place("ti", [P, NT, 8], U32)
        tif = place("tif", [P, NT, 2])
        io8 = place("io8", [P, E])
        io8i = place("io8i", [P, E], I32)
        thr = place("thr", [P, 15])
        thri = place("thri", [P, 15], I32)
        nm = place("nm", [P, NT])
        sm = place("sm", [P, NT])
        rc = place("rc", [P, NT])
        ez = place("ez", [P, NT])
        cnt = place("cnt", [P, E])
        cmpc = place("cmpc", [P, E, 15])
        nsl = place("nsl", [P, E])
        sst = place("sst", [P, E])
        posf = place("posf", [P, NT, 2])
        sio = place("sio", [1, 40])
        sioi = place("sioi", [1, 40], I32)
        scmp = place("scmp", [1, 40, 7])
        sexp = place("sexp", [1, 40])

        bank = [ctx.enter_context(nc.psum_tensor(f"bank{j}", [P, 512], F32)) for j in range(8)]
        bS, bT, bO, bM = bank[0:4], bank[4:6], bank[6], bank[7]
        bG, bU, bY = bank[0:2], bank[2:4], bank[4:8]
        bX3, bG3, bU3, bH3, bY3 = bank[0], bank[1:3], bank[3:5], bank[5], bank[6:8]

        g_const = sem("g_const")
        g_zero = sem("g_zero")
        ld_small = sem("ld_small")
        ld_x, ld_cn, ld_cd = sems("ld_x", 2), sems("ld_cn", 2), sems("ld_cd", 2)
        e_rg, d_rg = sem("e_rg"), sem("d_rg")
        d_stat, d_aggr, d_vare = sems("d_stat", 2), sems("d_aggr", 2), sems("d_vare", 2)
        g_rstd, g_xn, g_kh, g_kl = sems("g_rstd", 2), sem("g_xn"), sem("g_kh"), sem("g_kl")
        a_qh, d_ql = sem("a_qh"), sem("d_ql")
        e_vt, a_vh, d_vl = sem("e_vt"), sem("a_vh"), sem("d_vl")
        e_s, d_max, a_exp, d_rinv, g_pn = sem("e_s"), sem("d_max"), sem("a_exp"), sem("d_rinv"), sem("g_pn")
        e_t, a_pth, d_ptl, e_pv = sem("e_t"), sem("a_pth"), sem("d_ptl"), sem("e_pv")
        d_o1, d_o2 = sem("d_o1"), sem("d_o2")
        g_x2n, e_x2T, a_x2T, e_lg, a_lg = sem("g_x2n"), sem("e_x2T"), sem("a_x2T"), sem("e_lg"), sem("a_lg")
        st_x2, st_x2n, st_x2T = sems("st_x2", 2), sems("st_x2n", 2), sems("st_x2T", 2)
        st_pad = sem("st_pad")
        ld_stg, ld_x2T, ld_xr, st_out = sems("ld_stg", 2), sems("ld_x2T", 2), sems("ld_xr", 2), sems("st_out", 2)
        a_wh, d_wl, a_xh, d_xl = sem("a_wh"), sem("d_wl"), sem("a_xh"), sem("d_xl")
        e_g, e_u, e_d = sem("e_g"), sem("e_u"), sem("e_d")
        a_sg, d_hm, a_hh, d_hl, d_out = sem("a_sg"), sem("d_hm"), sem("a_hh"), sem("d_hl"), sem("d_out")
        d_r, a_r, e_r = sem("d_r"), sem("a_r"), sem("e_r")
        st_meta0, st_meta = sem("st_meta0"), sem("st_meta")
        ld_ex = sems("ld_ex", E)
        ld_mt, ld_xg, st_y = sems("ld_mt", 4), sems("ld_xg", 4), sems("st_y", 2)
        e_tx, a_xt, e_g3, e_u3, a_sl, d_h = sem("e_tx"), sem("a_xt"), sem("e_g3"), sem("e_u3"), sem("a_sl"), sem("d_h")
        e_th, d_ht, e_d3, a_y = sem("e_th"), sem("d_ht"), sem("e_d3"), sem("a_y")

        N_CONST = 13
        R_LS = 2
        R_M = R_LS + 8 + 2 * NT + 7
        R_EV = R_M + 2
        R_TAB = R_EV + NT + 1 + 3 + E + 3
        R_POS = R_TAB + 3 + 2 * TOPK + 1

        def after(eng, s, value):
            if not isinstance(value, int) or value > 0:
                eng.wait_ge(s, value)

        def wait_ahead(eng, s, value):
            if isinstance(value, int):
                if value <= 0:
                    return
            else:
                eng.compute_val(value)
                eng.wait_ge(g_const, N_CONST)
            eng.wait_ge(s, value)

        def over_tiles(eng, step):
            step(0, True, False)
            step(1, False, False)
            with eng.Fori(2, NI - 1) as i:
                step(i, False, False)
            step(NI - 1, False, True)

        def over_slots(eng, slot):
            for s in range(8):
                slot(s, s)
            with eng.Fori(2, SLOTS // 4) as i:
                for j in range(4):
                    slot(4 * i + j, j)
            for s in range(SLOTS // 4 * 4, SLOTS):
                slot(s, s)

        block = ctx.enter_context(nc.Block())

        @block.sync
        def _(sp):
            sp.dma_start(rg[0:E, :], router_w).then_inc(ld_small, 16)
            sp.dma_start(rg[E:NR, :], shared_gate_w.rearrange("(a h) -> a h", a=1)).then_inc(ld_small, 16)
            sp.dma_start(gam[:, :], gamma.partition_broadcast(P)).then_inc(ld_small, 16)

            def load_tile(t, par):
                after(sp, d_o1, 2 * t - 2)
                sp.dma_start(xb[par][:, :], x_t[t, :, :]).then_inc(ld_x[par], 16)
                after(sp, e_vt, t - 1)
                sp.dma_start(cn[par][:, :], c_t[t, :, :]).then_inc(ld_cn[par], 16)
                after(sp, g_kl, t - 1)
                for half in range(2):
                    sp.dma_start(cd[par][DH * half:DH * (half + 1), :, :], c_h[t, :, :, :]).then_inc(ld_cd[par], 16)

            def store_tile(t, par):
                after(sp, d_o2, 2 * t + 2)
                sp.dma_start(x2_t[t, :, :], x2b[par][:, :]).then_inc(st_x2[par], 16)
                after(sp, g_x2n, t + 1)
                sp.dma_start(xn_d[0:T, :].rearrange("(t p) h -> t p h", p=P)[t, :, :], x2n[par][:, :]).then_inc(st_x2n[par], 16)
                after(sp, a_x2T, t + 1)
                sp.dma_start(xT_d[t, :, :], x2T[par][:, :, :].rearrange("p c t -> p (c t)")).then_inc(st_x2T[par], 16)

            load_tile(0, 0)
            sp.wait_ge(g_zero, 1)
            sp.dma_start(out[T:T + P, :], zrow[:, :]).then_inc(st_pad, 16)
            sp.dma_start(xn_d[T:T + P, :], zrow[:, :]).then_inc(st_pad, 16)
            sp.wait_ge(g_const, N_CONST)
            sp.dma_start(meta_d.rearrange("(s p) c -> p s c", p=P), mini[:, :, :]).then_inc(st_meta0, 16)

            def step(i, first, last):
                for par in range(2):
                    t = 2 * i + par
                    if not (last and par == 1):
                        load_tile(t + 1, 1 - par)
                    if not (first and par == 0):
                        store_tile(t - 1, 1 - par)
            over_tiles(sp, step)

            g_c = sw_gate.rearrange("(h p) (c n) -> c p h n", p=P, n=P)
            u_c = sw_up.rearrange("(h p) (c n) -> c p h n", p=P, n=P)
            d_c = sw_down.rearrange("(c p) n -> c p n", p=P)

            def load_chunk(c):
                after(sp, d_wl, c - 1)
                for n, src in enumerate((g_c[c, :, :, :], u_c[c, :, :, :])):
                    sp.dma_start(stg[c % 2][:, n, :].rearrange("p (h n) -> p h n", h=HC), src).then_inc(ld_stg[c % 2], 16)
                sp.dma_start(stg[c % 2][:, 2, :], d_c[c, :, :]).then_inc(ld_stg[c % 2], 16)

            def load_block(b, par):
                for q in range(2):
                    sp.wait_ge(st_x2T[q], 16 * (TB * (b + 1) // 2))
                after(sp, e_u, SC * (b - 1))
                sp.dma_start(xl[:, par, :, :, :].bitcast(F32).rearrange("p t c n -> p t (c n)"),
                             xT_d.rearrange("(b t) p n -> b p t n", t=TB)[b, :, :, :]).then_inc(ld_x2T[par], 16)

            load_chunk(0)
            load_chunk(1)
            store_tile(NT - 1, 1)
            load_block(0, 0)
            load_block(1, 1)
            for c in range(2, SC):
                load_chunk(c)

            def load_rows(n, par):
                after(sp, st_out[par], 16 * (n // 2))
                sp.dma_start(xr[par][:, :], x2_t[n, :, :]).then_inc(ld_xr[par], 16)

            def store_out(n, par):
                sp.wait_ge(d_out, n + 1)
                sp.dma_start(out[0:T, :].rearrange("(t p) h -> t p h", p=P)[n, :, :], xr[par][:, :]).then_inc(st_out[par], 16)

            sp.wait_ge(st_x2[0], 16 * NI)
            sp.wait_ge(st_x2[1], 16 * NI)
            load_rows(0, 0)
            load_rows(1, 1)

            def outputs(b, more):
                for tt in range(TB):
                    n = TB * b + tt
                    store_out(n, tt % 2)
                    if tt < TB - 2 or more:
                        sp.wait_ge(st_out[tt % 2], 16 * (TB // 2 * b + tt // 2 + 1))
                        sp.dma_start(xr[tt % 2][:, :], x2_t[n + 2, :, :]).then_inc(ld_xr[tt % 2], 16)

            load_block(2, 0)
            outputs(0, True)
            load_block(3, 1)
            outputs(1, True)
            outputs(2, True)

            def load_expert(e):
                under = min(SC - 1, (EW * (e + 1) - 1) // (2 * WCH))
                sp.wait_ge(e_d, SC * (NB - 1) + under + 1)
                w = wex[:, e, :]
                sp.dma_start(w[:, 0:HC * I].rearrange("p (c i) -> p c i", c=HC),
                             w_gate[e, :, :].rearrange("(c p) i -> p c i", p=P)).then_inc(ld_ex[e], 16)
                sp.dma_start(w[:, HC * I:2 * HC * I].rearrange("p (c i) -> p c i", c=HC),
                             w_up[e, :, :].rearrange("(c p) i -> p c i", p=P)).then_inc(ld_ex[e], 16)
                sp.dma_start(w[:, 2 * HC * I:2 * HC * I + (IC - 1) * H].rearrange("p (c h) -> p c h", c=IC - 1),
                             w_down[e, 0:(IC - 1) * P, :].rearrange("(c p) h -> p c h", p=P)).then_inc(ld_ex[e], 16)
                sp.dma_start(w[0:IR, 2 * HC * I + (IC - 1) * H:EW], w_down[e, (IC - 1) * P:I, :]).then_inc(ld_ex[e], 16)

            for e in range(E - 1):
                load_expert(e)
            sp.wait_ge(st_meta, 16 * NT * TOPK)
            m_s = meta_d.rearrange("(s p) c -> s p c", p=P)
            for s in range(4):
                sp.dma_start(mt[s][:, :], m_s[s, :, :]).then_inc(ld_mt[s], 16)
            outputs(NB - 1, False)
            load_expert(E - 1)

            def meta_of(s, half, j):
                sp.wait_ge(st_y[j % 2], half)
                sp.dma_start(mt[j % 4][:, :], m_s[s + 4, :, :]).then_inc(ld_mt[j % 4], 16)

            for s in range(8):
                meta_of(s, 16 * (s // 2 + 1), s)
            with sp.Fori(2, SLOTS // 4 - 1) as i:
                for j in range(4):
                    meta_of(4 * i + j, 32 * i + 16 * (j // 2 + 1), j)
            for s in range((SLOTS // 4 - 1) * 4, SLOTS - 4):
                meta_of(s, 16 * (s // 2 + 1), s)
            sp.wait_ge(st_y[0], 16 * ((SLOTS + 1) // 2))
            sp.wait_ge(st_y[1], 16 * (SLOTS // 2))
            for q in range(2):
                sp.wait_ge(st_out[q], 16 * NI)
                sp.wait_ge(st_x2[q], 16 * NI)
                sp.wait_ge(st_x2n[q], 16 * NI)
                sp.wait_ge(st_x2T[q], 16 * NI)
            sp.wait_ge(st_pad, 32)
            sp.wait_ge(st_meta0, 16)

        @block.gpsimd
        def _(g):
            gp = nc.gpsimd
            made = [0]

            def const(ins):
                made[0] += 1
                ins.then_inc(g_const, 1)

            gp.memset(zrow[:, :], 0.0).then_inc(g_zero, 1)
            const(gp.memset(ident[:, :], 0.0))
            const(gp.memset(tri[:, :], 1.0))
            const(gp.memset(ones[:, :], 1.0))
            const(gp.memset(mhalf[:, :], -0.5))
            g.wait_ge(g_const, 4)
            const(gp.affine_select(out=ident[:, :], in_=ident[:, :], compare_op=ALU.not_equal, fill=1.0,
                                   base=0, pattern=[[-1, P]], channel_multiplier=1))
            const(gp.affine_select(out=tri[:, :], in_=tri[:, :], compare_op=ALU.is_gt, fill=0.0,
                                   base=0, pattern=[[1, P]], channel_multiplier=-1))
            const(gp.iota(mini[:, :, 0], pattern=[[0, SLOTS]], base=T, channel_multiplier=1))
            const(gp.memset(mini[:, :, 1], 0))
            for k in range(TOPK):
                const(gp.iota(msrc[:, :, k, 0], pattern=[[P, NT]], base=0, channel_multiplier=1))
            const(gp.iota(io8i[:, :], pattern=[[1, E]], base=0, channel_multiplier=0))
            const(gp.iota(thri[:, :], pattern=[[P, 15]], base=P, channel_multiplier=0))
            const(gp.iota(sioi[:, :], pattern=[[1, 40]], base=0, channel_multiplier=0))
            assert made[0] == N_CONST

            def power(k, n):
                g.wait_ge(d_vare[k], n + 1)
                gp.tensor_tensor(rstd[:, k, :], vare[:, k, :], mhalf[:, :], ALU.pow).then_inc(g_rstd[k], 1)
                wait_ahead(g, g_rstd[k], n + 1)

            def prep(t, half, par):
                power(0, t)
                wait_ahead(g, d_ql, 2 * t - 2)
                gp.tensor_scalar(xn[par][:, :], xb[par][:, :], aggr[:, 0, 0:1], rstd[:, 0, :],
                                 ALU.subtract, ALU.mult).then_inc(g_xn, 1)

            def keys_hi(t, half, par):
                wait_ahead(g, e_s, 4 * t - 4)
                wait_ahead(g, ld_cd[par], 32 * (half + 1))
                gp.tensor_scalar(kh[par][:, :, :], cd[par][:, :, :], 1.0, 0.0, ALU.mult, ALU.add).then_inc(g_kh, 1)
                g.wait_ge(g_kh, t + 1)

            def keys_lo(t, par):
                gp.tensor_tensor(kl[par][:, :, :], cd[par][:, :, :], kh[par][:, :, :].bitcast(F32), ALU.subtract).then_inc(g_kl, 1)

            def norm_p(k, s, pair):
                wait_ahead(g, d_rinv, 2 * k + pair + 1)
                for q in (2 * pair, 2 * pair + 1):
                    gp.tensor_scalar(pb[s][:, q, :], pb[s][:, q, :], rinv[:, s, q:q + 1], 0.0,
                                     ALU.mult, ALU.add).then_inc(g_pn, 1)

            def normed_rows(t, half, par):
                after(g, st_x2n[par], 16 * half)
                after(g, e_x2T, t - 1)
                power(1, t)
                gp.tensor_scalar(x2n[par][:, :], x2b[par][:, :], aggr[:, 1, 0:1], rstd[:, 1, :],
                                 ALU.subtract, ALU.mult).then_inc(g_x2n, 1)

            g.wait_ge(g_const, N_CONST)
            keys_hi(0, 0, 0)
            keys_lo(0, 0)
            prep(0, 0, 0)
            norm_p(0, 0, 0)
            norm_p(0, 0, 1)

            def step(i, first, last):
                for par in range(2):
                    t = 2 * i + par
                    nxt = 1 - par
                    nhalf = i + par
                    lhalf = i - 1 + par
                    final = last and par == 1
                    if not (first and par == 0):
                        normed_rows(t - 1, lhalf, nxt)
                    norm_p(2 * t + 1, 1, 0)
                    if not final:
                        prep(t + 1, nhalf, nxt)
                    norm_p(2 * t + 1, 1, 1)
                    if not final:
                        keys_hi(t + 1, nhalf, nxt)
                        keys_lo(t + 1, nxt)
                        norm_p(2 * t + 2, 0, 0)
                        norm_p(2 * t + 2, 0, 1)
            over_tiles(g, step)
            normed_rows(NT - 1, NI - 1, 1)

            g.wait_ge(d_r, R_POS)
            g.wait_ge(st_meta0, 16)
            for t in range(NT):
                for k in range(TOPK):
                    g.indirect_dma_start(out=meta_d, out_offset=bass.IndirectOffsetOnAxis(ap=posi[:, t, k:k + 1], axis=0),
                                         in_=msrc[:, t, k, :], in_offset=None).then_inc(st_meta, 16)
            g.wait_ge(st_x2n[0], 16 * NI)
            g.wait_ge(st_x2n[1], 16 * NI)
            g.wait_ge(st_pad, 32)

            def gather(s, turn, j):
                wait_ahead(g, e_tx, s - 3)
                wait_ahead(g, ld_mt[j % 4], 16 * (turn + 1))
                g.indirect_dma_start(out=xg[j % 4][:, :], out_offset=None, in_=xn_d,
                                     in_offset=bass.IndirectOffsetOnAxis(ap=mt[j % 4][:, 0:1], axis=0)).then_inc(ld_xg[j % 4], 16)

            def scatter(s, half, j):
                if isinstance(s, int) and s == 0:
                    g.wait_ge(st_out[0], 16 * NI)
                    g.wait_ge(st_out[1], 16 * NI)
                else:
                    wait_ahead(g, st_y[(j + 1) % 2], 16 * half)
                wait_ahead(g, a_y, s + 1)
                g.indirect_dma_start(out=out, out_offset=bass.IndirectOffsetOnAxis(ap=mt[j % 4][:, 0:1], axis=0),
                                     in_=y3[j % 2][:, :], in_offset=None, compute_op=ALU.add).then_inc(st_y[j % 2], 16)

            for s in range(3):
                gather(s, 0, s)
            for s in range(8):
                gather(s + 3, (s + 3) // 4, s + 3)
                scatter(s, (s + 1) // 2, s)
            with g.Fori(2, SLOTS // 4 - 1) as i:
                for j in range(4):
                    gather(4 * i + j + 3, i + (j + 3) // 4, j + 3)
                    scatter(4 * i + j, 2 * i + (j + 1) // 2, j)
            for s in range((SLOTS // 4 - 1) * 4, SLOTS):
                if s + 3 < SLOTS:
                    gather(s + 3, (s + 3) // 4, s + 3)
                scatter(s, (s + 1) // 2, s)

        @block.scalar
        def _(act):
            sc = nc.scalar

            def queries_hi(t, par):
                act.wait_ge(g_xn, t + 1)
                for s in range(2):
                    after(act, e_s, 2 * (2 * t - 2 + s) + 2)
                    r = slice(DH * s, DH * (s + 1))
                    sc.activation(qs[s][r, :], xn[par][r, :], ACT.Copy).then_inc(a_qh, 1)

            def values_hi(t, par):
                act.wait_ge(e_vt, t + 1)
                after(act, e_pv, 8 * t - 8)
                sc.activation(vs[par][:, :, :, 0, :], bM[:, :].rearrange("p (c s d) -> p c s d", c=LC, s=2),
                              ACT.Copy).then_inc(a_vh, 1)

            def exps(k, s, pair):
                act.wait_ge(d_max, 2 * k + pair + 1)
                for q in (2 * pair, 2 * pair + 1):
                    after(act, e_t, 4 * k - 4)
                    after(act, g_pn, 4 * k - 4)
                    sc.activation(pb[s][:, q, :], bS[q][:, :], ACT.Exp, bias=negmax[:, s, q:q + 1], scale=1.0,
                                  accum_out=rsum[:, s, q:q + 1]).then_inc(a_exp, 1)

            def probs_hi(k, c):
                act.wait_ge(e_t, 4 * k + c + 1)
                after(act, e_pv, 4 * k + c - 3)
                sc.activation(pth[c][:, :], bT[c % 2][:, :], ACT.Copy).then_inc(a_pth, 1)

            def rows_T(t, half, par):
                act.wait_ge(e_x2T, t + 1)
                after(act, st_x2T[par], 16 * half)
                after(act, e_lg, t - 1)
                sc.activation(x2T[par][:, :, :], bM[:, :].rearrange("p (c t) -> p c t", c=HC), ACT.Copy).then_inc(a_x2T, 1)

            def logits(t):
                act.wait_ge(e_lg, t + 1)
                sc.activation(lg_all[:, t, :], bM[:, 0:NR], ACT.Copy).then_inc(a_lg, 1)

            values_hi(0, 0)
            queries_hi(0, 0)
            exps(0, 0, 0)
            exps(0, 0, 1)

            def step(i, first, last):
                for par in range(2):
                    t = 2 * i + par
                    final = last and par == 1
                    k = 2 * t
                    probs_hi(k, 0)
                    probs_hi(k, 1)
                    exps(k + 1, 1, 0)
                    probs_hi(k, 2)
                    if not final:
                        values_hi(t + 1, 1 - par)
                    exps(k + 1, 1, 1)
                    probs_hi(k, 3)
                    if not final:
                        queries_hi(t + 1, 1 - par)
                    k = 2 * t + 1
                    probs_hi(k, 0)
                    probs_hi(k, 1)
                    if not final:
                        exps(k + 1, 0, 0)
                    probs_hi(k, 2)
                    if not (first and par == 0):
                        rows_T(t - 1, i - 1 + par, 1 - par)
                    if not final:
                        exps(k + 1, 0, 1)
                    probs_hi(k, 3)
                    if not (first and par == 0):
                        logits(t - 1)
            over_tiles(act, step)
            rows_T(NT - 1, NI - 1, 1)
            logits(NT - 1)

            act.wait_ge(e_lg, NT)
            act.wait_ge(g_x2n, NT)
            act.wait_ge(a_lg, NT)
            act.wait_ge(d_o2, 2 * NT)
            for q in range(2):
                act.wait_ge(st_x2[q], 16 * NI)
                act.wait_ge(st_x2n[q], 16 * NI)
                act.wait_ge(st_x2T[q], 16 * NI)
            act.wait_ge(st_pad, 32)

            def weights_hi(c):
                act.wait_ge(ld_stg[c % 2], 48 * (c // 2 + 1))
                sc.activation(wsp[c][:, 0, :], stg[c % 2][:, :, :].rearrange("p a n -> p (a n)"), ACT.Copy).then_inc(a_wh, 1)

            def tokens_hi(b, par):
                act.wait_ge(ld_x2T[par], 16 * (b // 2 + 1) if isinstance(b, int) else 16)
                after(act, e_u, SC * (b - 1))
                sc.activation(xh[:, par, :, :, :], xl[:, par, :, :, :].bitcast(F32), ACT.Copy).then_inc(a_xh, 1)

            def silu_hi(b, c):
                n = SC * b + c
                p = c % 2
                act.wait_ge(e_g, n + 1)
                prev = n if c == 0 else n - 1
                after(act, d_hl, prev)
                sc.activation(sg[p][:, :], bG[p][:, :], ACT.Silu).then_inc(a_sg, 1)

            def hidden_hi(b, c):
                n = SC * b + c
                p = c % 2
                act.wait_ge(d_hm, n + 1)
                after(act, e_d, n if c == 0 else n - 1)
                sc.activation(hh[p][:, :], sg[p][:, :], ACT.Copy).then_inc(a_hh, 1)

            weights_hi(0)
            tokens_hi(0, 0)
            weights_hi(1)
            for c in range(SC):
                silu_hi(0, c)
                if c + 2 < SC:
                    weights_hi(c + 2)
                if c == 5:
                    tokens_hi(1, 1)
                hidden_hi(0, c)
            act.wait_ge(d_r, R_LS)
            sc.activation(ls[:, :, :], ls[:, :, :], ACT.Exp).then_inc(a_r, 1)
            sc.activation(ez[:, :], lg_all[:, :, E], ACT.Exp, scale=-1.0).then_inc(a_r, 1)
            for b in range(1, NB):
                for c in range(SC):
                    silu_hi(b, c)
                    if c == 5 and b + 1 < NB:
                        tokens_hi(b + 1, (b + 1) % 2)
                    hidden_hi(b, c)

            act.wait_ge(e_u, SC * NB)

            def rows3(s, j):
                act.wait_ge(e_tx, s + 1)
                after(act, e_u3, s - 1)
                sc.activation(xT3[j % 2][:, :, :], bX3[:, :].rearrange("p (c t) -> p c t", c=HC), ACT.Copy).then_inc(a_xt, 1)

            def silu3(s, j):
                act.wait_ge(e_g3, s + 1)
                after(act, e_th, s - 1)
                sc.activation(h3[j % 2][:, :], bG3[j % 2][:, 0:I], ACT.Silu).then_inc(a_sl, 1)

            def weigh(s, half, j):
                act.wait_ge(e_d3, s + 1)
                after(act, st_y[j % 2], 16 * half)
                sc.activation(y3[j % 2][:, :], bY3[j % 2][:, :], ACT.Copy,
                              scale=mt[j % 4][:, 1:2].bitcast(F32)).then_inc(a_y, 1)

            rows3(0, 0)
            rows3(1, 1)
            silu3(0, 0)

            def slot(s, j):
                if not (isinstance(s, int) and s + 2 >= SLOTS):
                    rows3(s + 2, j + 2)
                if not (isinstance(s, int) and s + 1 >= SLOTS):
                    silu3(s + 1, j + 1)

            for s in range(8):
                slot(s, s)
                weigh(s, s // 2, s)
            with act.Fori(2, SLOTS // 4) as i:
                for j in range(4):
                    slot(4 * i + j, j)
                    weigh(4 * i + j, 2 * i + j // 2, j)
            for s in range(SLOTS // 4 * 4, SLOTS):
                slot(s, s)
                weigh(s, s // 2, s)

        @block.vector
        def _(dve):
            ve = nc.vector

            def moments(kind, n, src, scale):
                after(dve, (g_xn, g_x2n)[kind], n)
                ve.bn_stats(stats[:, kind, :], src).then_inc(d_stat[kind], 1)
                wait_ahead(dve, d_stat[kind], n + 1)
                ve.bn_aggr(aggr[:, kind, :], stats[:, kind, :]).then_inc(d_aggr[kind], 1)
                dve.wait_ge(d_aggr[kind], n + 1)
                ve.tensor_scalar(vare[:, kind, :], aggr[:, kind, 1:2], scale, scale * EPS, ALU.mult, ALU.add).then_inc(d_vare[kind], 1)

            def first_norm(t, half, par):
                dve.wait_ge(ld_x[par], 16 * (half + 1))
                moments(0, t, xb[par][:, :], float(DH))

            def values_lo(t, par):
                dve.wait_ge(a_vh, t + 1)
                ve.tensor_tensor(vs[par][:, :, :, 1, :], bM[:, :].rearrange("p (c s d) -> p c s d", c=LC, s=2),
                                 vs[par][:, :, :, 0, :].bitcast(F32), ALU.subtract).then_inc(d_vl, 1)

            def queries_lo(t, par):
                for s in range(2):
                    dve.wait_ge(a_qh, 2 * t + s + 1)
                    r = slice(DH * s, DH * (s + 1))
                    o = slice(DH * (1 - s), DH * (2 - s))
                    ve.tensor_tensor(qs[s][o, :], xn[par][r, :], qs[s][r, :].bitcast(F32), ALU.subtract).then_inc(d_ql, 1)

            def maxima(k, s, pair):
                dve.wait_ge(e_s, 2 * k + pair + 1)
                after(dve, a_exp, 4 * k - 4)
                for q in (2 * pair, 2 * pair + 1):
                    ins = ve.tensor_reduce(negmax[:, s, q:q + 1], bS[q][:, :], AX_X, ALU.max, negate=True)
                ins.then_inc(d_max, 1)

            def inverse(k, s, pair):
                dve.wait_ge(a_exp, 4 * k + 2 * pair + 2)
                after(dve, g_pn, 4 * k - 4)
                ve.reciprocal(rinv[:, s, 2 * pair:2 * pair + 2], rsum[:, s, 2 * pair:2 * pair + 2]).then_inc(d_rinv, 1)

            def probs_lo(k, c):
                dve.wait_ge(a_pth, 4 * k + c + 1)
                ve.tensor_tensor(ptl[c][:, :], bT[c % 2][:, :], pth[c][:, :].bitcast(F32), ALU.subtract).then_inc(d_ptl, 1)

            def head_out(t, half, s, par):
                k = 2 * t + s
                dve.wait_ge(e_pv, 4 * k + 4)
                r = slice(DH * s, DH * (s + 1))
                if s == 0:
                    after(dve, st_x2[par], 16 * half)
                    after(dve, g_x2n, t - 1)
                ve.scalar_tensor_tensor(x2b[par][r, :], bO[0:DH, :], gam[0:DH, :], xb[par][r, :], ALU.mult, ALU.add).then_inc(d_o1, 1)
                dve.wait_ge(d_o1, k + 1)
                ve.scalar_tensor_tensor(x2b[par][r, :], bO[DH:P, :], gam[DH:P, :], x2b[par][r, :], ALU.mult, ALU.add).then_inc(d_o2, 1)

            dve.wait_ge(e_rg, 1)
            ve.tensor_copy(rgT[:, :, :], bM[:, 0:HC * NR].rearrange("p (c n) -> p c n", c=HC)).then_inc(d_rg, 1)
            dve.wait_ge(g_const, N_CONST)
            first_norm(0, 0, 0)
            values_lo(0, 0)
            queries_lo(0, 0)
            maxima(0, 0, 0)
            maxima(0, 0, 1)
            inverse(0, 0, 0)
            inverse(0, 0, 1)

            def step(i, first, last):
                for par in range(2):
                    t = 2 * i + par
                    final = last and par == 1
                    nhalf = i + par
                    k = 2 * t
                    if not (first and par == 0):
                        dve.wait_ge(d_o2, 2 * t)
                        moments(1, t - 1, x2b[1 - par][:, :], 1.0)
                    probs_lo(k, 0)
                    maxima(k + 1, 1, 0)
                    probs_lo(k, 1)
                    maxima(k + 1, 1, 1)
                    if not final:
                        first_norm(t + 1, nhalf, 1 - par)
                    probs_lo(k, 2)
                    inverse(k + 1, 1, 0)
                    if not final:
                        values_lo(t + 1, 1 - par)
                    probs_lo(k, 3)
                    head_out(t, i, 0, par)
                    inverse(k + 1, 1, 1)
                    if not final:
                        queries_lo(t + 1, 1 - par)
                    k = 2 * t + 1
                    probs_lo(k, 0)
                    if not final:
                        maxima(k + 1, 0, 0)
                    probs_lo(k, 1)
                    if not final:
                        maxima(k + 1, 0, 1)
                    probs_lo(k, 2)
                    if not final:
                        inverse(k + 1, 0, 0)
                    probs_lo(k, 3)
                    head_out(t, i, 1, par)
                    if not final:
                        inverse(k + 1, 0, 1)
            over_tiles(dve, step)
            dve.wait_ge(d_o2, 2 * NT)
            moments(1, NT - 1, x2b[1][:, :], 1.0)

            def weights_lo(c):
                dve.wait_ge(a_wh, c + 1)
                ve.tensor_tensor(wsp[c][:, 1, :], stg[c % 2][:, :, :].rearrange("p a n -> p (a n)"),
                                 wsp[c][:, 0, :].bitcast(F32), ALU.subtract).then_inc(d_wl, 1)

            def tokens_lo(b, par):
                dve.wait_ge(a_xh, b + 1)
                v = xl[:, par, :, :, :]
                ve.tensor_tensor(v, v.bitcast(F32), xh[:, par, :, :, :].bitcast(F32), ALU.subtract).then_inc(d_xl, 1)

            def hidden(b, c):
                n = SC * b + c
                p = c % 2
                dve.wait_ge(a_sg, n + 1)
                dve.wait_ge(e_u, n + 1)
                ve.tensor_tensor(sg[p][:, :], bU[p][:, :], sg[p][:, :], ALU.mult).then_inc(d_hm, 1)
                dve.wait_ge(a_hh, n + 1)
                ve.tensor_tensor(hl[p][:, :], sg[p][:, :], hh[p][:, :].bitcast(F32), ALU.subtract).then_inc(d_hl, 1)

            def outputs(b):
                dve.wait_ge(e_d, SC * (b + 1))
                for tt in range(TB):
                    n = TB * b + tt
                    dve.wait_ge(ld_xr[tt % 2], 16 * (n // 2 + 1))
                    ve.scalar_tensor_tensor(xr[tt % 2][:, :], bY[tt][:, :], sig[:, n:n + 1], xr[tt % 2][:, :],
                                            ALU.mult, ALU.add).then_inc(d_out, 1)

            weights_lo(0)
            tokens_lo(0, 0)
            weights_lo(1)
            for c in range(SC):
                hidden(0, c)
                if c + 2 < SC:
                    weights_lo(c + 2)
                if c == 5:
                    tokens_lo(1, 1)

            done = [0]

            def step_r(ins, wait=True):
                done[0] += 1
                ins.then_inc(d_r, 1)
                if wait:
                    dve.wait_ge(d_r, done[0])

            def bc(ap, shape):
                return ap.to_broadcast(shape)

            full = [P, NT, E]
            dve.wait_ge(a_lg, NT)
            lgv = lg_all[:, :, 0:E]
            step_r(ve.tensor_reduce(nm[:, :], lgv, AX_X, ALU.max, negate=True))
            step_r(ve.tensor_tensor(ls[:, :, :], lgv, bc(nm[:, :].unsqueeze(2), full), ALU.add))
            assert done[0] == R_LS
            step_r(ve.tensor_copy(io8[:, :], io8i[:, :]))
            step_r(ve.tensor_copy(thr[:, :], thri[:, :]))
            step_r(ve.tensor_copy(sio[:, :], sioi[:, :]))
            dve.wait_ge(a_r, 2)
            step_r(ve.tensor_reduce(sm[:, :], ls[:, :, :], AX_X, ALU.add))
            step_r(ve.reciprocal(rc[:, :], sm[:, :]))
            step_r(ve.tensor_tensor(ls[:, :, :], ls[:, :, :], bc(rc[:, :].unsqueeze(2), full), ALU.mult))
            step_r(ve.tensor_scalar(ez[:, :], ez[:, :], 1.0, None, ALU.add))
            step_r(ve.reciprocal(sig[:, :], ez[:, :]))
            for t in range(NT):
                step_r(ve.max(tv[:, t, :], ls[:, t, :]), False)
            dve.wait_ge(d_r, done[0])
            for t in range(NT):
                step_r(ve.max_index(ti[:, t, :], tv[:, t, :], ls[:, t, :]), False)
            step_r(ve.tensor_tensor(sm[:, :], tv[:, :, 0], tv[:, :, 1], ALU.add))
            step_r(ve.reciprocal(rc[:, :], sm[:, :]))
            step_r(ve.tensor_tensor(msrc[:, :, :, 1].bitcast(F32), tv[:, :, 0:2], bc(rc[:, :].unsqueeze(2), [P, NT, 2]), ALU.mult))
            step_r(ve.tensor_copy(tif[:, :, :], ti[:, :, 0:2]))
            for k, m in enumerate((m1, m2)):
                step_r(ve.tensor_tensor(m[:, :, :], bc(tif[:, :, k:k + 1], full), bc(io8[:, :].unsqueeze(1), full), ALU.is_equal))
            step_r(ve.tensor_tensor(ls[:, :, :], m1[:, :, :], m2[:, :, :], ALU.add))
            assert done[0] == R_M, done[0]
            outputs(0)
            dve.wait_ge(e_r, 1)
            step_r(ve.tensor_copy(pre_s[:, :, :], bY[0][:, 0:P].rearrange("p (t e) -> p t e", e=E)), False)
            step_r(ve.tensor_copy(tot_s[:, :, :], bY[0][:, P:2 * P].rearrange("p (t e) -> p t e", e=E)))
            assert done[0] == R_EV, done[0]
            step_r(ve.memset(carry[:, 0, :], 0.0))
            for t in range(1, NT):
                step_r(ve.tensor_tensor(carry[:, t, :], carry[:, t - 1, :], tot_s[:, t - 1, :], ALU.add))
            step_r(ve.tensor_tensor(cnt[:, :], carry[:, NT - 1, :], tot_s[:, NT - 1, :], ALU.add))
            step_r(ve.tensor_tensor(cmpc[:, :, :], bc(cnt[:, :].unsqueeze(2), [P, E, 15]), bc(thr[:, :].unsqueeze(1), [P, E, 15]), ALU.is_gt))
            step_r(ve.tensor_reduce(nsl[:, :], cmpc[:, :, :], AX_X, ALU.add))
            step_r(ve.tensor_scalar(nsl[:, :], nsl[:, :], 1.0, None, ALU.add))
            step_r(ve.memset(sst[:, 0:1], 0.0))
            for e in range(1, E):
                step_r(ve.tensor_tensor(sst[:, e:e + 1], sst[:, e - 1:e], nsl[:, e - 1:e], ALU.add))
            step_r(ve.tensor_tensor(scmp[:, :, :], bc(sio[:, :].unsqueeze(2), [1, 40, 7]), bc(sst[0:1, 1:E].unsqueeze(1), [1, 40, 7]), ALU.is_ge))
            step_r(ve.tensor_reduce(sexp[:, :], scmp[:, :, :], AX_X, ALU.add))
            step_r(ve.tensor_copy(slot_tab[:, :], sexp[:, :]))
            assert done[0] == R_TAB, done[0]
            step_r(ve.tensor_scalar(sst[:, :], sst[:, :], float(P), None, ALU.mult))
            step_r(ve.tensor_tensor(pre_s[:, :, :], pre_s[:, :, :], carry[:, :, :], ALU.add))
            step_r(ve.tensor_tensor(pre_s[:, :, :], pre_s[:, :, :], bc(sst[:, :].unsqueeze(1), full), ALU.add))
            for k, m in enumerate((m1, m2)):
                step_r(ve.tensor_tensor(m[:, :, :], m[:, :, :], pre_s[:, :, :], ALU.mult))
                step_r(ve.tensor_reduce(posf[:, :, k], m[:, :, :], AX_X, ALU.add))
            step_r(ve.tensor_copy(posi[:, :, :], posf[:, :, :]))
            assert done[0] == R_POS, done[0]

            for b in range(1, NB):
                for c in range(SC):
                    hidden(b, c)
                    if c == 0 and b > 1:
                        outputs(b - 1)
                    if c == 5 and b + 1 < NB:
                        tokens_lo(b + 1, (b + 1) % 2)
            outputs(NB - 1)

            def hidden3(s, j):
                dve.wait_ge(a_sl, s + 1)
                dve.wait_ge(e_u3, s + 1)
                ve.tensor_tensor(h3[j % 2][:, :], bU3[j % 2][:, 0:I], h3[j % 2][:, :], ALU.mult).then_inc(d_h, 1)

            def hidden_T3(s, j):
                dve.wait_ge(e_th, s + 1)
                after(dve, e_d3, s - 1)
                ve.tensor_copy(hT3[j % 2][:, 0:IC - 1, :], bH3[:, 0:(IC - 1) * P].rearrange("p (c t) -> p c t", c=IC - 1)).then_inc(d_ht, 1)
                ve.tensor_copy(hT3[j % 2][0:IR, IC - 1, :], bH3[0:IR, (IC - 1) * P:IC * P]).then_inc(d_ht, 1)

            hidden3(0, 0)

            def slot(s, j):
                if not (isinstance(s, int) and s + 1 >= SLOTS):
                    hidden3(s + 1, j + 1)
                hidden_T3(s, j)
            over_slots(dve, slot)

        @block.tensor
        def _(pe):
            te = nc.tensor

            pe.wait_ge(ld_small, 48)
            pe.wait_ge(g_const, N_CONST)
            for c in range(HC):
                ins = te.transpose(bM[:, c * NR:(c + 1) * NR], rg[:, c * P:(c + 1) * P], ident[0:NR, 0:NR])
            ins.then_inc(e_rg, 1)

            def scores(k, t, par, s, pair):
                if pair == 0:
                    pe.wait_ge(d_ql, k + 1)
                    pe.wait_ge(g_kl, t + 1)
                after(pe, a_exp, 4 * k - 4 + 2 * pair + 2)
                for q in (2 * pair, 2 * pair + 1):
                    te.matmul(bS[q][:, :], qs[s][:, q * P:(q + 1) * P], kh[par][:, s, :], start=True, stop=False)
                    ins = te.matmul(bS[q][:, :], qs[s][:, q * P:(q + 1) * P], kl[par][:, s, :], start=False, stop=True)
                ins.then_inc(e_s, 1)

            def probs_T(k, s, c):
                if c == 0:
                    pe.wait_ge(g_pn, 4 * k + 4)
                after(pe, d_ptl, 4 * k + c - 1)
                for q in range(QC):
                    ins = te.transpose(bT[c % 2][:, q * P:(q + 1) * P], pb[s][:, q, c * P:(c + 1) * P], ident[:, :])
                ins.then_inc(e_t, 1)

            def times_v(k, s, par, c):
                if c == 0:
                    after(pe, d_o2, k)
                pe.wait_ge(a_pth, 4 * k + c + 1)
                te.matmul(bO[:, :], vs[par][:, c, s, :, :].rearrange("p a d -> p (a d)"), pth[c][:, :], start=(c == 0), stop=False)
                pe.wait_ge(d_ptl, 4 * k + c + 1)
                te.matmul(bO[:, :], vs[par][:, c, s, :, :].rearrange("p a d -> p (a d)"), ptl[c][:, :],
                          start=False, stop=(c == LC - 1)).then_inc(e_pv, 1)

            def values_T(t, half, par):
                pe.wait_ge(ld_cn[par], 16 * (half + 1))
                if isinstance(t, int) and t < 2:
                    pe.wait_ge(d_rg, 1)
                if isinstance(t, int) and t == 2:
                    pe.wait_ge(d_vl, 2)
                after(pe, a_lg, t - 2)
                for c in range(LC):
                    ins = te.transpose(bM[:, c * P:(c + 1) * P], cn[par][:, c * P:(c + 1) * P], ident[:, :])
                ins.then_inc(e_vt, 1)

            def rows_T(t, par):
                pe.wait_ge(g_x2n, t + 1)
                if isinstance(t, int) and t + 2 >= NT:
                    pe.wait_ge(a_lg, t)
                else:
                    pe.wait_ge(d_vl, t + 3)
                for c in range(HC):
                    ins = te.transpose(bM[:, c * P:(c + 1) * P], x2n[par][:, c * P:(c + 1) * P], ident[:, :])
                ins.then_inc(e_x2T, 1)

            def logits(t, par):
                pe.wait_ge(a_x2T, t + 1)
                for c in range(HC):
                    ins = te.matmul(bM[:, 0:NR], x2T[par][:, c, :], rgT[:, c, :], start=(c == 0), stop=(c == HC - 1))
                ins.then_inc(e_lg, 1)

            values_T(0, 0, 0)
            scores(0, 0, 0, 0, 0)
            scores(0, 0, 0, 0, 1)
            pe.wait_ge(d_vl, 1)

            def step(i, first, last):
                for par in range(2):
                    t = 2 * i + par
                    final = last and par == 1
                    k = 2 * t
                    scores(k + 1, t, par, 1, 0)
                    probs_T(k, 0, 0)
                    probs_T(k, 0, 1)
                    scores(k + 1, t, par, 1, 1)
                    if not final:
                        values_T(t + 1, i + par, 1 - par)
                    pe.wait_ge(d_vl, t + 1)
                    times_v(k, 0, par, 0)
                    probs_T(k, 0, 2)
                    times_v(k, 0, par, 1)
                    probs_T(k, 0, 3)
                    times_v(k, 0, par, 2)
                    times_v(k, 0, par, 3)
                    k = 2 * t + 1
                    if not final:
                        scores(k + 1, t + 1, 1 - par, 0, 0)
                    probs_T(k, 1, 0)
                    probs_T(k, 1, 1)
                    if not final:
                        scores(k + 1, t + 1, 1 - par, 0, 1)
                    times_v(k, 1, par, 0)
                    if not (first and par == 0):
                        rows_T(t - 1, 1 - par)
                    probs_T(k, 1, 2)
                    times_v(k, 1, par, 1)
                    probs_T(k, 1, 3)
                    times_v(k, 1, par, 2)
                    if not (first and par == 0):
                        logits(t - 1, 1 - par)
                    times_v(k, 1, par, 3)
            over_tiles(pe, step)
            rows_T(NT - 1, 1)
            logits(NT - 1, 1)

            def gate_up(b, c, par):
                n = SC * b + c
                p = c % 2
                prev = n if c == 0 else n - 1
                if c == 0:
                    pe.wait_ge(d_xl, b + 1)
                if isinstance(b, int) and b == 0:
                    pe.wait_ge(d_wl, c + 1)
                w = wsp[c]
                for name, (bk, used, s_out) in enumerate(((bG[p], a_sg, e_g), (bU[p], d_hm, e_u))):
                    after(pe, used, prev)
                    for h in range(HC):
                        hi = w[:, 0, name * 512 + h * P:name * 512 + (h + 1) * P]
                        lo = w[:, 1, name * 512 + h * P:name * 512 + (h + 1) * P]
                        xhi, xlo = xh[:, par, :, h, :], xl[:, par, :, h, :]
                        te.matmul(bk[:, :], hi, xhi, start=(h == 0), stop=False)
                        te.matmul(bk[:, :], hi, xlo, start=False, stop=False)
                        ins = te.matmul(bk[:, :], lo, xhi, start=False, stop=(h == HC - 1))
                    ins.then_inc(s_out, 1)

            def down(b, c):
                n = SC * b + c
                p = c % 2
                pe.wait_ge(d_hl, n + 1)
                hi, lo = wsp[c][:, 0, 1024:1536], wsp[c][:, 1, 1024:1536]
                for tt in range(TB):
                    if c == 0:
                        after(pe, d_out, TB * b - TB + tt + 1)
                    th, tl = hh[p][:, tt * P:(tt + 1) * P], hl[p][:, tt * P:(tt + 1) * P]
                    te.matmul(bY[tt][:, :], th, hi, start=(c == 0), stop=False)
                    te.matmul(bY[tt][:, :], th, lo, start=False, stop=False)
                    ins = te.matmul(bY[tt][:, :], tl, hi, start=False, stop=(c == SC - 1))
                ins.then_inc(e_d, 1)

            def block2(b, par, last):
                for c in range(1, SC):
                    gate_up(b, c, par)
                    down(b, c - 1)
                if not last:
                    gate_up(b + 1, 0, 1 - par)
                down(b, SC - 1)

            pe.wait_ge(a_lg, NT)
            gate_up(0, 0, 0)
            block2(0, 0, False)
            pe.wait_ge(d_r, R_M)
            pe.wait_ge(d_out, TB)
            te.matmul(bY[0][:, 0:P], tri[:, :], ls[:, :, :].rearrange("p t e -> p (t e)"), start=True, stop=True)
            te.matmul(bY[0][:, P:2 * P], ones[:, :], ls[:, :, :].rearrange("p t e -> p (t e)"), start=True, stop=True).then_inc(e_r, 1)
            pe.wait_ge(d_r, R_EV)
            for b in range(1, NB):
                block2(b, b % 2, b == NB - 1)

            def rows3(s, turn, j):
                pe.wait_ge(ld_xg[j % 4], 16 * (turn + 1))
                after(pe, a_xt, s)
                for c in range(HC):
                    ins = te.transpose(bX3[:, c * P:(c + 1) * P], xg[j % 4][:, c * P:(c + 1) * P], ident[:, :])
                ins.then_inc(e_tx, 1)

            def gate_up3(s, j):
                if isinstance(s, int) and s < E:
                    pe.wait_ge(ld_ex[s], 64)
                e = te.value_load(slot_tab[0:1, s:s + 1] if isinstance(s, int) else slot_tab[0:1, bass.ds(s, 1)], min_val=0, max_val=E - 1)
                pe.wait_ge(a_xt, s + 1)
                for m, (bk, used, s_out) in enumerate(((bG3[j % 2], a_sl, e_g3), (bU3[j % 2], d_h, e_u3))):
                    after(pe, used, s - 1)
                    for c in range(HC):
                        ins = te.matmul(bk[:, 0:I], xT3[j % 2][:, c, :], wex[:, e, (m * HC + c) * I:(m * HC + c + 1) * I],
                                        start=(c == 0), stop=(c == HC - 1))
                    ins.then_inc(s_out, 1)
                return e

            def down3(s, j, e):
                pe.wait_ge(d_h, s + 1)
                after(pe, d_ht, 2 * s)
                for c in range(IC):
                    w = P if c < IC - 1 else IR
                    ins = te.transpose(bH3[0:w, c * P:(c + 1) * P], h3[j % 2][:, c * P:c * P + w], ident[:, :])
                ins.then_inc(e_th, 1)
                pe.wait_ge(d_ht, 2 * s + 2)
                after(pe, a_y, s - 1)
                for c in range(IC):
                    w = P if c < IC - 1 else IR
                    o = 2 * HC * I + c * H
                    ins = te.matmul(bY3[j % 2][:, :], hT3[j % 2][0:w, c, :], wex[0:w, e, o:o + H], start=(c == 0), stop=(c == IC - 1))
                ins.then_inc(e_d3, 1)

            pe.wait_ge(d_r, R_TAB)
            pe.wait_ge(d_out, NT)
            rows3(0, 0, 0)
            rows3(1, 0, 1)
            gate_up3(0, 0)

            def expert_of(s):
                return te.value_load(slot_tab[0:1, s:s + 1] if isinstance(s, int) else slot_tab[0:1, bass.ds(s, 1)], min_val=0, max_val=E - 1)

            def slot(s, turn, j):
                if not (isinstance(s, int) and s + 2 >= SLOTS):
                    rows3(s + 2, turn, j + 2)
                if not (isinstance(s, int) and s + 1 >= SLOTS):
                    gate_up3(s + 1, j + 1)
                down3(s, j, expert_of(s))

            for s in range(8):
                slot(s, (s + 2) // 4, s)
            with pe.Fori(2, SLOTS // 4) as i:
                for j in range(4):
                    slot(4 * i + j, i + (j + 2) // 4, j)
            for s in range(SLOTS // 4 * 4, SLOTS):
                slot(s, (s + 2) // 4, s)


def kernel(**inputs):
    import numpy as np
    import concourse.bacc as bacc
    from concourse.bass_utils import run_bass_kernel_spmd

    names = ["x", "ctx_2048", "L0_xattn_gamma", "L0_ffn_router_w", "L0_ffn_w_gate", "L0_ffn_w_up", "L0_ffn_w_down",
             "L0_ffn_sw_gate", "L0_ffn_sw_up", "L0_ffn_sw_down", "L0_ffn_shared_gate_w"]
    nc = bacc.Bacc("TRN2", target_bir_lowering=False, num_devices=1)
    arrays, args = {}, []
    for name in names:
        a = np.ascontiguousarray(inputs[name])
        if a.ndim == 0:
            a = a.reshape(1)
        arrays[f"in_{name}"] = a
        args.append(nc.dram_tensor(f"in_{name}", a.shape, mybir.dt.from_np(a.dtype), kind="ExternalInput").ap())
    shape = inputs["x"].shape
    rows = shape[0] * shape[1]
    args.append(nc.dram_tensor("out", (rows + P, shape[2]), F32, kind="ExternalOutput").ap())
    xattn_moe_kernel(nc, *args)
    r = run_bass_kernel_spmd(nc, [arrays], core_ids=[0])
    return r.results[0]["out"][:rows].reshape(shape)
```

```python
from contextlib import ExitStack

import concourse.bass as bass
from concourse import mybir

ALU = mybir.AluOpType
ACT = mybir.ActivationFunctionType
AX_X = mybir.AxisListType.X
F32 = mybir.dt.float32
F32R = mybir.dt.float32r
I32 = mybir.dt.int32
U32 = mybir.dt.uint32

P = 128
EPS = 1e-5


def xattn_moe_kernel(nc, x, ctx_in, gamma, router_w, w_gate, w_up, w_down, sw_gate, sw_up, sw_down, shared_gate_w, out):
    B, D, L = x.shape
    NH = 8
    DH = D // NH
    T = B * D
    H = L
    E, _, I = w_gate.shape
    SI = sw_gate.shape[1]
    NT = T // P
    HC = H // P
    LC = L // P
    QC = L // P
    NB = T // 512
    TB = 512 // P
    SC = SI // P
    IC = (I + P - 1) // P
    IR = I - (IC - 1) * P
    TOPK = 2
    SLOTS = (TOPK * T + (P - 1) * E) // P
    NR = E + 1
    NI = NT // 2
    assert DH == 64 and D == 512 and L == 512 and SI % P == 0 and NT % 2 == 0 and SLOTS == 39

    x_t = x.rearrange("b d l -> (b d) l").rearrange("(t p) l -> t p l", p=P)
    c_t = ctx_in.rearrange("b d l -> (b d) l").rearrange("(t p) l -> t p l", p=P)
    c_h = ctx_in.rearrange("b d l -> (b d) l").rearrange("(t s p) l -> t p s l", s=2, p=DH)
    x2_d = nc.dram_tensor("x2_rows", (T, H), F32, kind="Internal").ap()
    x2_t = x2_d.rearrange("(t p) h -> t p h", p=P)
    xn_d = nc.dram_tensor("x2_normed_rows", (T + P, H), F32, kind="Internal").ap()
    xT_d = nc.dram_tensor("x2_normed_transposed", (NT, P, H), F32, kind="Internal").ap()
    meta_d = nc.dram_tensor("slot_rows", (SLOTS * P, 2), I32, kind="Internal").ap()

    ctx = ExitStack()
    with ctx:
        def sem(name):
            return ctx.enter_context(nc.semaphore(name))

        def sems(name, n):
            return [sem(f"{name}{j}") for j in range(n)]

        base = (nc.sbuf_base + 31) // 32 * 32
        cursor = [base]

        def place(name, shape, dt=F32):
            n = 4
            for d in shape[1:]:
                n *= d
            t = nc.alloc_sbuf_tensor_at(name, list(shape), dt, offset=cursor[0])
            cursor[0] += (n + 31) // 32 * 32
            assert cursor[0] <= nc.sbuf_usable_end, (name, cursor[0])
            return t

        ident = place("ident", [P, P])
        tri = place("tri", [P, P])
        ones = place("ones", [P, P])
        rgT = place("rgT", [P, HC, NR])
        gam = place("gam", [P, 1])
        mhalf = place("mhalf", [P, 1])
        lg_all = place("lg_all", [P, NT, NR])
        sig = place("sig", [P, NT])
        posi = place("posi", [P, NT, TOPK], I32)
        msrc = place("msrc", [P, NT, TOPK, 2], I32)
        slot_tab = place("slot_tab", [1, 40], I32)
        meta = place("meta", [P, SLOTS, 2], I32)
        stats = place("stats", [P, 2, 6])
        aggr = place("aggr", [P, 2, 2])
        vare = place("vare", [P, 2, 1])
        rstd = place("rstd", [P, 2, 1])
        nmr = place("nmr", [P, 2, 1])
        negmax = place("negmax", [P, 2, QC])
        rsum = place("rsum", [P, 2, QC])
        rinv = place("rinv", [P, 2, QC])
        gidx = [place(f"gidx{j}", [P, 1], I32) for j in range(4)]
        sidx = [place(f"sidx{j}", [P, 1], I32) for j in range(4)]
        fixed_end = cursor[0]

        WCH = 3 * 512
        EW = 2 * HC * I + IC * H
        big = cursor[0]
        xb = [place(f"xb{j}", [P, L]) for j in range(2)]
        cn = [place(f"cn{j}", [P, L]) for j in range(2)]
        cd = [place(f"cd{j}", [P, 2, L]) for j in range(2)]
        kh = [place(f"kh{j}", [P, 2, L], F32R) for j in range(2)]
        kl = [place(f"kl{j}", [P, 2, L], F32R) for j in range(2)]
        xn = [place(f"xn{j}", [P, L]) for j in range(2)]
        qs = [place(f"qs{j}", [P, L], F32R) for j in range(2)]
        vs = [place(f"vs{j}", [P, 2, LC, 3, DH], F32R) for j in range(2)]
        pb = [place(f"pb{j}", [P, QC, L]) for j in range(2)]
        pth = [place(f"pth{j}", [P, L], F32R) for j in range(4)]
        ptl = [place(f"ptl{j}", [P, L], F32R) for j in range(4)]
        x2b = [place(f"x2b{j}", [P, L]) for j in range(2)]
        x2n = [place(f"x2n{j}", [P, H]) for j in range(2)]
        x2T = [place(f"x2T{j}", [P, HC, P]) for j in range(2)]
        rg = place("rg", [NR, H])
        zrow = place("zrow", [P, H])
        stage1_end = cursor[0]
        cursor[0] = big
        wsp = [place(f"wsp{c}", [P, 2, WCH], F32R) for c in range(SC)]
        cursor[0] = big
        wex = place("wex", [P, E, EW])
        big_end = cursor[0]
        assert stage1_end <= big_end
        stg0 = cursor[0]
        stg = [place(f"stg{j}", [P, 3, 512]) for j in range(2)]
        stg_end = cursor[0]
        xhl0 = cursor[0]
        xh = place("xh", [P, 2, TB, HC, P], F32R)
        xl = place("xl", [P, 2, TB, HC, P], F32R)
        sg = [place(f"sg{j}", [P, 512]) for j in range(2)]
        hh = [place(f"hh{j}", [P, 512], F32R) for j in range(2)]
        hl = [place(f"hl{j}", [P, 512], F32R) for j in range(2)]
        xr = [place(f"xr{j}", [P, H]) for j in range(2)]
        tables0 = cursor[0]
        cursor[0] = stg0
        xg = [place(f"xg{j}", [P, H]) for j in range(4)]
        xr += [place(f"xr{j}", [P, H]) for j in (2, 3)]
        assert cursor[0] <= stg_end
        cursor[0] = xhl0
        xT3 = [place(f"xT3{j}", [P, HC, P]) for j in range(2)]
        h3 = [place(f"h3{j}", [P, I]) for j in range(2)]
        hT3 = [place(f"hT3{j}", [P, IC, P]) for j in range(2)]
        y3 = [place(f"y3{j}", [P, H]) for j in range(2)]
        assert cursor[0] <= xhl0 + 4 * 2048 * 2
        cursor[0] = tables0
        ls = place("ls", [P, NT, E])
        pre_s = place("pre_s", [P, NT, E])
        tot_s = place("tot_s", [P, NT, E])
        carry = place("carry", [P, NT, E])
        m1 = place("m1", [P, NT, E])
        m2 = place("m2", [P, NT, E])
        tv = place("tv", [P, NT, 8])
        ti = place("ti", [P, NT, 8], U32)
        tif = place("tif", [P, NT, 2])
        io8 = place("io8", [P, E])
        io8i = place("io8i", [P, E], I32)
        thr = place("thr", [P, 15])
        thri = place("thri", [P, 15], I32)
        nm = place("nm", [P, NT])
        sm = place("sm", [P, NT])
        rc = place("rc", [P, NT])
        ez = place("ez", [P, NT])
        cnt = place("cnt", [P, E])
        cmpc = place("cmpc", [P, E, 15])
        nsl = place("nsl", [P, E])
        sst = place("sst", [P, E])
        posf = place("posf", [P, NT, 2])
        sio = place("sio", [1, 40])
        sioi = place("sioi", [1, 40], I32)
        scmp = place("scmp", [1, 40, 7])
        sexp = place("sexp", [1, 40])

        bank = [ctx.enter_context(nc.psum_tensor(f"bank{j}", [P, 512], F32)) for j in range(8)]
        bS, bT, bO, bM = bank[0:4], bank[4:6], bank[6], bank[7]
        bG, bU, bY = bank[0:2], bank[2:4], bank[4:8]
        bX3, bG3, bU3, bH3, bY3 = bank[0], bank[1:3], bank[3:5], bank[5], bank[6:8]

        g_const = sem("g_const")
        g_zero = sem("g_zero")
        ld_small = sem("ld_small")
        ld_x, ld_cn, ld_cd, ld_x2 = sems("ld_x", 2), sems("ld_cn", 2), sems("ld_cd", 2), sems("ld_x2", 2)
        e_rg, d_rg = sem("e_rg"), sem("d_rg")
        d_stat, d_aggr, d_vare = sems("d_stat", 2), sems("d_aggr", 2), sems("d_vare", 2)
        g_rstd, g_nmr, a_xn, g_kh, g_kl = sems("g_rstd", 2), sems("g_nmr", 2), sem("a_xn"), sem("g_kh"), sem("g_kl")
        a_qh, g_ql = sem("a_qh"), sem("g_ql")
        e_vt, a_vh, d_vl = sem("e_vt"), sem("a_vh"), sem("d_vl")
        e_s, d_max, a_exp, d_rinv, g_pn = sem("e_s"), sem("d_max"), sem("a_exp"), sem("d_rinv"), sem("g_pn")
        e_t, a_pth, d_ptl, e_pv = sem("e_t"), sem("a_pth"), sem("d_ptl"), sem("e_pv")
        d_x2 = sem("d_x2")
        a_x2n, e_x2T, a_x2T, e_lg, a_lg = sem("a_x2n"), sem("e_x2T"), sem("a_x2T"), sem("e_lg"), sem("a_lg")
        st_x2, st_x2n, st_x2T = sems("st_x2", 2), sems("st_x2n", 2), sems("st_x2T", 2)
        st_pad = sem("st_pad")
        ld_stg, ld_x2T, ld_xr, st_out = sems("ld_stg", 2), sems("ld_x2T", 2), sems("ld_xr", TB), sems("st_out", TB)
        a_wh, d_wl, a_xh, d_xl = sem("a_wh"), sem("d_wl"), sem("a_xh"), sem("d_xl")
        e_g, e_u, e_d = sem("e_g"), sem("e_u"), sem("e_d")
        a_sg, d_hm, a_hh, d_hl, d_out = sem("a_sg"), sem("d_hm"), sem("a_hh"), sem("d_hl"), sem("d_out")
        d_r, a_r, e_r = sem("d_r"), sem("a_r"), sem("e_r")
        st_meta0, st_meta = sem("st_meta0"), sem("st_meta")
        ld_ex = sems("ld_ex", E)
        ld_meta, ld_xg, st_y = sem("ld_meta"), sems("ld_xg", 4), sems("st_y", 2)
        g_gi, g_si = sem("g_gi"), sem("g_si")
        e_tx, a_xt, e_g3, e_u3, a_sl, d_h = sem("e_tx"), sem("a_xt"), sem("e_g3"), sem("e_u3"), sem("a_sl"), sem("d_h")
        e_th, d_ht, e_d3, a_y = sem("e_th"), sem("d_ht"), sem("e_d3"), sem("a_y")

        N_CONST = 15
        R_LS = 2
        R_M = R_LS + 8 + 2 * NT + 7
        R_EV = R_M + 2
        R_TAB = R_EV + NT + 1 + 3 + E + 3
        R_POS = R_TAB + 3 + 2 * TOPK + 1

        def after(eng, s, value):
            if not isinstance(value, int) or value > 0:
                eng.wait_ge(s, value)

        def wait_ahead(eng, s, value):
            if isinstance(value, int):
                if value <= 0:
                    return
            else:
                eng.compute_val(value)
                eng.wait_ge(g_const, N_CONST)
            eng.wait_ge(s, value)

        def there(t):
            return not isinstance(t, int) or 0 <= t < NT

        def over_tiles(eng, tile):
            for i in (0, 1):
                for par in range(2):
                    tile(2 * i + par, i, par)
            with eng.Fori(2, NI - 1) as i:
                for par in range(2):
                    tile(2 * i + par, i, par)
            for par in range(2):
                tile(2 * (NI - 1) + par, NI - 1, par)

        def over_slots(eng, slot):
            for s in range(8):
                slot(s, s)
            with eng.Fori(2, SLOTS // 4) as i:
                for j in range(4):
                    slot(4 * i + j, j)
            for s in range(SLOTS // 4 * 4, SLOTS):
                slot(s, s)

        block = ctx.enter_context(nc.Block())

        @block.sync
        def _(sp):
            def load_x(t, par):
                after(sp, a_xn, t - 1)
                sp.dma_start(xb[par][:, :], x_t[t, :, :]).then_inc(ld_x[par], 16)

            def load_keys(t, par):
                after(sp, g_kl, t - 1)
                for half in range(2):
                    sp.dma_start(cd[par][DH * half:DH * (half + 1), :, :], c_h[t, :, :, :]).then_inc(ld_cd[par], 16)

            def load_values(t, par):
                after(sp, e_vt, t - 1)
                sp.dma_start(cn[par][:, :], c_t[t, :, :]).then_inc(ld_cn[par], 16)

            def load_x2(t, half, par):
                if not isinstance(t, int):
                    sp.compute_val(16 * half)
                after(sp, a_x2n, t - 1)
                after(sp, st_x2[par], 16 * half)
                sp.dma_start(x2b[par][:, :], x_t[t, :, :]).then_inc(ld_x2[par], 16)

            def store_rows(t, par):
                sp.wait_ge(d_x2, t + 1)
                sp.dma_start(x2_t[t, :, :], x2b[par][:, :]).then_inc(st_x2[par], 16)
                sp.wait_ge(a_x2n, t + 1)
                sp.dma_start(xn_d[0:T, :].rearrange("(t p) h -> t p h", p=P)[t, :, :], x2n[par][:, :]).then_inc(st_x2n[par], 16)

            def store_columns(t, par):
                sp.wait_ge(a_x2T, t + 1)
                sp.dma_start(xT_d[t, :, :], x2T[par][:, :, :].rearrange("p c t -> p (c t)")).then_inc(st_x2T[par], 16)

            load_x(0, 0)
            load_keys(0, 0)
            load_values(0, 0)
            load_x(1, 1)
            load_keys(1, 1)
            load_values(1, 1)
            load_x2(0, 0, 0)
            sp.dma_start(rg[0:E, :], router_w).then_inc(ld_small, 16)
            sp.dma_start(rg[E:NR, :], shared_gate_w.rearrange("(a h) -> a h", a=1)).then_inc(ld_small, 16)
            sp.dma_start(gam[:, :], gamma.partition_broadcast(P)).then_inc(ld_small, 16)
            sp.wait_ge(g_zero, 1)
            sp.dma_start(out[T:T + P, :], zrow[:, :]).then_inc(st_pad, 16)
            sp.dma_start(xn_d[T:T + P, :], zrow[:, :]).then_inc(st_pad, 16)
            sp.wait_ge(g_const, N_CONST)
            sp.dma_start(meta_d.rearrange("(s p) c -> p s c", p=P), meta[:, :, :]).then_inc(st_meta0, 16)

            g_c = sw_gate.rearrange("(h p) (c n) -> c p h n", p=P, n=P)
            u_c = sw_up.rearrange("(h p) (c n) -> c p h n", p=P, n=P)
            d_c = sw_down.rearrange("(c p) n -> c p n", p=P)

            def load_chunk(c):
                after(sp, d_wl, c - 1)
                for n, src in enumerate((g_c[c, :, :, :], u_c[c, :, :, :])):
                    sp.dma_start(stg[c % 2][:, n, :].rearrange("p (h n) -> p h n", h=HC), src).then_inc(ld_stg[c % 2], 16)
                sp.dma_start(stg[c % 2][:, 2, :], d_c[c, :, :]).then_inc(ld_stg[c % 2], 16)

            def load_block(b, par):
                for q in range(2):
                    sp.wait_ge(st_x2T[q], 16 * (TB * (b + 1) // 2))
                after(sp, e_u, SC * (b - 1))
                sp.dma_start(xl[:, par, :, :, :].bitcast(F32).rearrange("p t c n -> p t (c n)"),
                             xT_d.rearrange("(b t) p n -> b p t n", t=TB)[b, :, :, :]).then_inc(ld_x2T[par], 16)

            def tile(t, i, par):
                if there(t + 2):
                    load_x(t + 2, par)
                    load_keys(t + 2, par)
                if there(t - 2):
                    store_columns(t - 2, par)
                if there(t - 1):
                    store_rows(t - 1, 1 - par)
                if there(t + 1):
                    load_x2(t + 1, i + par, 1 - par)
                if there(t + 2):
                    load_values(t + 2, par)
                if isinstance(t, int) and t == NT - 2:
                    load_chunk(0)
                    load_chunk(1)
                    load_block(0, 0)
                    load_block(1, 1)
            over_tiles(sp, tile)

            store_columns(NT - 2, 0)
            store_rows(NT - 1, 1)
            store_columns(NT - 1, 1)
            for c in range(2, SC):
                load_chunk(c)

            def load_rows(b):
                for tt in range(TB):
                    after(sp, st_out[tt], 16 * b)
                    sp.dma_start(xr[tt][:, :], x2_t[TB * b + tt, :, :]).then_inc(ld_xr[tt], 16)

            def store_out(b):
                for tt in range(TB):
                    n = TB * b + tt
                    sp.wait_ge(d_out, n + 1)
                    sp.dma_start(out[0:T, :].rearrange("(t p) h -> t p h", p=P)[n, :, :], xr[tt][:, :]).then_inc(st_out[tt], 16)

            for q in range(2):
                sp.wait_ge(st_x2[q], 16 * NI)
            sp.wait_ge(d_wl, SC)
            load_rows(0)
            load_block(2, 0)
            store_out(0)
            load_rows(1)
            load_block(3, 1)
            store_out(1)
            load_rows(2)
            sp.wait_ge(st_meta, 16 * NT * TOPK)
            sp.dma_start(meta[:, :, :], meta_d.rearrange("(s p) c -> p s c", p=P)).then_inc(ld_meta, 16)
            store_out(2)
            load_rows(3)

            def load_expert(e):
                under = min(SC - 1, (EW * (e + 1) - 1) // (2 * WCH))
                sp.wait_ge(e_d, SC * (NB - 1) + under + 1)
                w = wex[:, e, :]
                sp.dma_start(w[:, 0:HC * I].rearrange("p (c i) -> p c i", c=HC),
                             w_gate[e, :, :].rearrange("(c p) i -> p c i", p=P)).then_inc(ld_ex[e], 16)
                sp.dma_start(w[:, HC * I:2 * HC * I].rearrange("p (c i) -> p c i", c=HC),
                             w_up[e, :, :].rearrange("(c p) i -> p c i", p=P)).then_inc(ld_ex[e], 16)
                sp.dma_start(w[:, 2 * HC * I:2 * HC * I + (IC - 1) * H].rearrange("p (c h) -> p c h", c=IC - 1),
                             w_down[e, 0:(IC - 1) * P, :].rearrange("(c p) h -> p c h", p=P)).then_inc(ld_ex[e], 16)
                sp.dma_start(w[0:IR, 2 * HC * I + (IC - 1) * H:EW], w_down[e, (IC - 1) * P:I, :]).then_inc(ld_ex[e], 16)

            for e in range(E - 1):
                load_expert(e)
            store_out(NB - 1)
            load_expert(E - 1)
            sp.wait_ge(st_y[0], 16 * ((SLOTS + 1) // 2))
            sp.wait_ge(st_y[1], 16 * (SLOTS // 2))
            for tt in range(TB):
                sp.wait_ge(st_out[tt], 16 * NB)
            for q in range(2):
                sp.wait_ge(st_x2[q], 16 * NI)
                sp.wait_ge(st_x2n[q], 16 * NI)
                sp.wait_ge(st_x2T[q], 16 * NI)
            sp.wait_ge(st_pad, 32)
            sp.wait_ge(st_meta0, 16)

        @block.gpsimd
        def _(g):
            gp = nc.gpsimd
            made = [0]

            def const(ins):
                made[0] += 1
                ins.then_inc(g_const, 1)

            gp.memset(zrow[:, :], 0.0).then_inc(g_zero, 1)
            const(gp.memset(ident[:, :], 0.0))
            const(gp.memset(tri[:, :], 1.0))
            const(gp.memset(ones[:, :], 1.0))
            const(gp.memset(mhalf[:, :], -0.5))
            for par in range(2):
                const(gp.memset(vs[par][:, :, :, 1, :].bitcast(F32), 0.0))
            g.wait_ge(g_const, 6)
            const(gp.affine_select(out=ident[:, :], in_=ident[:, :], compare_op=ALU.not_equal, fill=1.0,
                                   base=0, pattern=[[-1, P]], channel_multiplier=1))
            const(gp.affine_select(out=tri[:, :], in_=tri[:, :], compare_op=ALU.is_gt, fill=0.0,
                                   base=0, pattern=[[1, P]], channel_multiplier=-1))
            const(gp.iota(meta[:, :, 0], pattern=[[0, SLOTS]], base=T, channel_multiplier=1))
            const(gp.memset(meta[:, :, 1], 0))
            for k in range(TOPK):
                const(gp.iota(msrc[:, :, k, 0], pattern=[[P, NT]], base=0, channel_multiplier=1))
            const(gp.iota(io8i[:, :], pattern=[[1, E]], base=0, channel_multiplier=0))
            const(gp.iota(thri[:, :], pattern=[[P, 15]], base=P, channel_multiplier=0))
            const(gp.iota(sioi[:, :], pattern=[[1, 40]], base=0, channel_multiplier=0))
            assert made[0] == N_CONST

            def power(kind, n):
                after(g, (a_xn, a_x2n)[kind], n)
                g.wait_ge(d_vare[kind], n + 1)
                gp.tensor_tensor(rstd[:, kind, :], vare[:, kind, :], mhalf[:, :], ALU.pow).then_inc(g_rstd[kind], 1)
                wait_ahead(g, g_rstd[kind], n + 1)
                gp.tensor_scalar(nmr[:, kind, :], aggr[:, kind, 0:1], rstd[:, kind, :], -1.0, ALU.mult, ALU.mult).then_inc(g_nmr[kind], 1)

            def queries_lo(t, s, par, before, count):
                g.wait_ge(before, count)
                g.wait_ge(a_qh, 2 * t + s + 1)
                r = slice(DH * s, DH * (s + 1))
                o = slice(DH * (1 - s), DH * (2 - s))
                gp.tensor_tensor(qs[s][o, :], xn[par][r, :], qs[s][r, :].bitcast(F32), ALU.subtract).then_inc(g_ql, 1)
                wait_ahead(g, g_ql, 2 * t + s + 1)

            def keys_hi(t, half, par):
                wait_ahead(g, e_s, 4 * t - 4)
                wait_ahead(g, ld_cd[par], 32 * (half + 1))
                gp.tensor_scalar(kh[par][:, :, :], cd[par][:, :, :], 1.0, 0.0, ALU.mult, ALU.add).then_inc(g_kh, 1)

            def keys_lo(t, par):
                g.wait_ge(g_kh, t + 1)
                gp.tensor_tensor(kl[par][:, :, :], cd[par][:, :, :], kh[par][:, :, :].bitcast(F32), ALU.subtract).then_inc(g_kl, 1)

            def norm_p(k, s, pair):
                wait_ahead(g, d_rinv, 2 * k + pair + 1)
                for q in (2 * pair, 2 * pair + 1):
                    gp.tensor_scalar(pb[s][:, q, :], pb[s][:, q, :], rinv[:, s, q:q + 1], 0.0,
                                     ALU.mult, ALU.add).then_inc(g_pn, 1)

            g.wait_ge(g_const, N_CONST)
            power(0, 0)
            keys_hi(0, 0, 0)
            keys_lo(0, 0)
            queries_lo(0, 0, 0, g_kl, 1)
            queries_lo(0, 1, 0, g_ql, 1)
            power(0, 1)
            norm_p(0, 0, 0)
            norm_p(0, 0, 1)
            keys_hi(1, 0, 1)
            keys_lo(1, 1)
            queries_lo(1, 0, 1, g_kl, 2)

            def tile(t, i, par):
                k = 2 * t
                norm_p(k + 1, 1, 0)
                if there(t + 2):
                    keys_hi(t + 2, i + 1, par)
                norm_p(k + 1, 1, 1)
                if there(t - 1):
                    power(1, t - 1)
                if there(t + 1):
                    if there(t - 1):
                        queries_lo(t + 1, 1, 1 - par, g_nmr[1], t)
                    else:
                        queries_lo(t + 1, 1, 1 - par, g_pn, 4 * k + 8)
                if there(t + 2):
                    power(0, t + 2)
                if there(t + 1):
                    norm_p(k + 2, 0, 0)
                if there(t + 2):
                    keys_lo(t + 2, par)
                if there(t + 1):
                    norm_p(k + 2, 0, 1)
                if there(t + 2):
                    queries_lo(t + 2, 0, par, g_pn, 4 * k + 12)
            over_tiles(g, tile)
            power(1, NT - 1)

            g.wait_ge(d_r, R_POS)
            g.wait_ge(st_meta0, 16)
            for t in range(NT):
                for k in range(TOPK):
                    g.indirect_dma_start(out=meta_d, out_offset=bass.IndirectOffsetOnAxis(ap=posi[:, t, k:k + 1], axis=0),
                                         in_=msrc[:, t, k, :], in_offset=None).then_inc(st_meta, 16)
            g.wait_ge(st_x2n[0], 16 * NI)
            g.wait_ge(st_x2n[1], 16 * NI)
            g.wait_ge(st_pad, 32)

            g.wait_ge(ld_meta, 16)
            g.wait_ge(d_wl, SC)

            def gather(s, turn, j):
                wait_ahead(g, ld_xg[j % 4], 16 * turn)
                gp.tensor_copy(gidx[j % 4][:, :], meta[:, s, 0:1]).then_inc(g_gi, 1)
                wait_ahead(g, e_tx, s - 3)
                wait_ahead(g, g_gi, s + 1)
                g.indirect_dma_start(out=xg[j % 4][:, :], out_offset=None, in_=xn_d,
                                     in_offset=bass.IndirectOffsetOnAxis(ap=gidx[j % 4][:, 0:1], axis=0)).then_inc(ld_xg[j % 4], 16)

            def scatter(s, half, j):
                gp.tensor_copy(sidx[j % 4][:, :], meta[:, s, 0:1]).then_inc(g_si, 1)
                if isinstance(s, int) and s == 0:
                    for tt in range(TB):
                        g.wait_ge(st_out[tt], 16 * NB)
                else:
                    wait_ahead(g, st_y[(j + 1) % 2], 16 * half)
                wait_ahead(g, a_y, s + 1)
                wait_ahead(g, g_si, s + 1)
                g.indirect_dma_start(out=out, out_offset=bass.IndirectOffsetOnAxis(ap=sidx[j % 4][:, 0:1], axis=0),
                                     in_=y3[j % 2][:, :], in_offset=None, compute_op=ALU.add).then_inc(st_y[j % 2], 16)

            for s in range(3):
                gather(s, 0, s)
            for s in range(8):
                gather(s + 3, (s + 3) // 4, s + 3)
                scatter(s, (s + 1) // 2, s)
            with g.Fori(2, SLOTS // 4 - 1) as i:
                for j in range(4):
                    gather(4 * i + j + 3, i + (j + 3) // 4, j + 3)
                    scatter(4 * i + j, 2 * i + (j + 1) // 2, j)
            for s in range((SLOTS // 4 - 1) * 4, SLOTS):
                if s + 3 < SLOTS:
                    gather(s + 3, (s + 3) // 4, s + 3)
                scatter(s, (s + 1) // 2, s)

        @block.scalar
        def _(act):
            sc = nc.scalar

            def normed(kind, t, half, par):
                act.wait_ge(g_nmr[kind], t + 1)
                if kind == 0:
                    after(act, g_ql, 2 * t - 2)
                    sc.activation(xn[par][:, :], xb[par][:, :], ACT.Identity, bias=nmr[:, 0, :], scale=rstd[:, 0, :]).then_inc(a_xn, 1)
                else:
                    after(act, st_x2n[par], 16 * half)
                    after(act, e_x2T, t - 1)
                    sc.activation(x2n[par][:, :], x2b[par][:, :], ACT.Identity, bias=nmr[:, 1, :], scale=rstd[:, 1, :]).then_inc(a_x2n, 1)

            def queries_hi(t, s, par):
                act.wait_ge(a_xn, t + 1)
                after(act, e_s, 2 * (2 * t - 2 + s) + 2)
                r = slice(DH * s, DH * (s + 1))
                sc.activation(qs[s][r, :], xn[par][r, :], ACT.Copy).then_inc(a_qh, 1)

            def values_hi(t, par):
                act.wait_ge(e_vt, t + 1)
                after(act, e_pv, 8 * t - 8)
                sc.activation(vs[par][:, 0, :, 0:3:2, :], bM[:, :].rearrange("p (c s d) -> p c s d", c=LC, s=2),
                              ACT.Copy).then_inc(a_vh, 1)

            def exps(k, s, pair):
                act.wait_ge(d_max, 2 * k + pair + 1)
                for q in (2 * pair, 2 * pair + 1):
                    after(act, e_t, 4 * k - 4)
                    after(act, g_pn, 4 * k - 4)
                    sc.activation(pb[s][:, q, :], bS[q][:, :], ACT.Exp, bias=negmax[:, s, q:q + 1], scale=1.0,
                                  accum_out=rsum[:, s, q:q + 1]).then_inc(a_exp, 1)

            def probs_hi(k, c):
                act.wait_ge(e_t, 4 * k + c + 1)
                after(act, e_pv, 4 * k + c - 3)
                sc.activation(pth[c][:, :], bT[c % 2][:, :], ACT.Copy).then_inc(a_pth, 1)

            def rows_T(t, half, par):
                act.wait_ge(e_x2T, t + 1)
                after(act, st_x2T[par], 16 * half)
                after(act, e_lg, t - 1)
                sc.activation(x2T[par][:, :, :], bM[:, :].rearrange("p (c t) -> p c t", c=HC), ACT.Copy).then_inc(a_x2T, 1)

            def logits(t):
                act.wait_ge(e_lg, t + 1)
                sc.activation(lg_all[:, t, :], bM[:, 0:NR], ACT.Copy).then_inc(a_lg, 1)

            normed(0, 0, 0, 0)
            queries_hi(0, 0, 0)
            queries_hi(0, 1, 0)
            values_hi(0, 0)
            normed(0, 1, 0, 1)
            exps(0, 0, 0)
            exps(0, 0, 1)
            queries_hi(1, 0, 1)
            exps(1, 1, 0)

            def weights_hi(c):
                act.wait_ge(ld_stg[c % 2], 48 * (c // 2 + 1))
                sc.activation(wsp[c][:, 0, :], stg[c % 2][:, :, :].rearrange("p a n -> p (a n)"), ACT.Copy).then_inc(a_wh, 1)

            def tokens_hi(b, par):
                act.wait_ge(ld_x2T[par], 16 * (b // 2 + 1) if isinstance(b, int) else 16)
                after(act, e_u, SC * (b - 1))
                sc.activation(xh[:, par, :, :, :], xl[:, par, :, :, :].bitcast(F32), ACT.Copy).then_inc(a_xh, 1)

            def tile(t, i, par):
                k = 2 * t
                probs_hi(k, 0)
                probs_hi(k, 1)
                exps(k + 1, 1, 1)
                if there(t + 1):
                    queries_hi(t + 1, 1, 1 - par)
                probs_hi(k, 2)
                probs_hi(k, 3)
                if there(t + 1):
                    exps(k + 2, 0, 0)
                if there(t - 2):
                    logits(t - 2)
                k = 2 * t + 1
                probs_hi(k, 0)
                probs_hi(k, 1)
                if there(t - 1):
                    normed(1, t - 1, i - 1 + par, 1 - par)
                if there(t + 1):
                    exps(k + 1, 0, 1)
                if there(t + 2):
                    normed(0, t + 2, i + 1, par)
                    queries_hi(t + 2, 0, par)
                probs_hi(k, 2)
                if there(t + 1):
                    values_hi(t + 1, 1 - par)
                probs_hi(k, 3)
                if there(t + 1):
                    exps(k + 2, 1, 0)
                if there(t - 1):
                    rows_T(t - 1, i - 1 + par, 1 - par)
                if isinstance(t, int) and t == NT - 1:
                    tokens_hi(0, 0)
                    act.wait_ge(a_xn, NT)
                    act.wait_ge(e_vt, NT)
                    act.wait_ge(g_kl, NT)
                    weights_hi(0)
                    act.wait_ge(e_s, 4 * NT)
                    weights_hi(1)
            over_tiles(act, tile)
            logits(NT - 2)
            normed(1, NT - 1, NI - 1, 1)
            rows_T(NT - 1, NI - 1, 1)
            logits(NT - 1)

            act.wait_ge(e_lg, NT)
            act.wait_ge(a_x2n, NT)
            act.wait_ge(a_lg, NT)
            act.wait_ge(d_x2, NT)
            for q in range(2):
                act.wait_ge(st_x2[q], 16 * NI)
                act.wait_ge(st_x2n[q], 16 * NI)
                act.wait_ge(st_x2T[q], 16 * NI)
            act.wait_ge(st_pad, 32)

            def silu_hi(b, c):
                n = SC * b + c
                p = c % 2
                act.wait_ge(e_g, n + 1)
                prev = n if c == 0 else n - 1
                after(act, d_hl, prev)
                sc.activation(sg[p][:, :], bG[p][:, :], ACT.Silu).then_inc(a_sg, 1)

            def hidden_hi(b, c):
                n = SC * b + c
                p = c % 2
                act.wait_ge(d_hm, n + 1)
                after(act, e_d, n if c == 0 else n - 1)
                sc.activation(hh[p][:, :], sg[p][:, :], ACT.Copy).then_inc(a_hh, 1)

            for c in range(SC):
                silu_hi(0, c)
                if c + 2 < SC:
                    weights_hi(c + 2)
                if c == 5:
                    tokens_hi(1, 1)
                hidden_hi(0, c)
                if c == 1:
                    act.wait_ge(d_r, R_LS)
                    sc.activation(ls[:, :, :], ls[:, :, :], ACT.Exp).then_inc(a_r, 1)
                    sc.activation(ez[:, :], lg_all[:, :, E], ACT.Exp, scale=-1.0).then_inc(a_r, 1)
            for b in range(1, NB):
                for c in range(SC):
                    silu_hi(b, c)
                    if c == 5 and b + 1 < NB:
                        tokens_hi(b + 1, (b + 1) % 2)
                    hidden_hi(b, c)

            act.wait_ge(e_u, SC * NB)

            def rows3(s, j):
                act.wait_ge(e_tx, s + 1)
                after(act, e_u3, s - 1)
                sc.activation(xT3[j % 2][:, :, :], bX3[:, :].rearrange("p (c t) -> p c t", c=HC), ACT.Copy).then_inc(a_xt, 1)

            def silu3(s, j):
                act.wait_ge(e_g3, s + 1)
                after(act, e_th, s - 1)
                sc.activation(h3[j % 2][:, :], bG3[j % 2][:, 0:I], ACT.Silu).then_inc(a_sl, 1)

            def weigh(s, half, j):
                act.wait_ge(e_d3, s + 1)
                after(act, st_y[j % 2], 16 * half)
                sc.activation(y3[j % 2][:, :], bY3[j % 2][:, :], ACT.Copy,
                              scale=meta[:, s, 1:2].bitcast(F32)).then_inc(a_y, 1)

            rows3(0, 0)
            rows3(1, 1)
            silu3(0, 0)

            def slot(s, j):
                if not (isinstance(s, int) and s + 2 >= SLOTS):
                    rows3(s + 2, j + 2)
                if not (isinstance(s, int) and s + 1 >= SLOTS):
                    silu3(s + 1, j + 1)

            for s in range(8):
                slot(s, s)
                weigh(s, s // 2, s)
            with act.Fori(2, SLOTS // 4) as i:
                for j in range(4):
                    slot(4 * i + j, j)
                    weigh(4 * i + j, 2 * i + j // 2, j)
            for s in range(SLOTS // 4 * 4, SLOTS):
                slot(s, s)
                weigh(s, s // 2, s)

        @block.vector
        def _(dve):
            ve = nc.vector

            def moments(kind, n, src):
                ve.bn_stats(stats[:, kind, :], src).then_inc(d_stat[kind], 1)

            def aggregate(kind, n):
                wait_ahead(dve, g_nmr[kind], n)
                wait_ahead(dve, d_stat[kind], n + 1)
                ve.bn_aggr(aggr[:, kind, :], stats[:, kind, :]).then_inc(d_aggr[kind], 1)

            def variance(kind, n):
                dve.wait_ge(d_aggr[kind], n + 1)
                scale = (float(DH), 1.0)[kind]
                ve.tensor_scalar(vare[:, kind, :], aggr[:, kind, 1:2], scale, scale * EPS, ALU.mult, ALU.add).then_inc(d_vare[kind], 1)

            def first_norm(t, half, par):
                dve.wait_ge(ld_x[par], 16 * (half + 1))
                moments(0, t, xb[par][:, :])

            def values_lo(t, par):
                dve.wait_ge(a_vh, t + 1)
                ve.tensor_tensor(vs[par][:, 1, :, 0:3:2, :], bM[:, :].rearrange("p (c s d) -> p c s d", c=LC, s=2),
                                 vs[par][:, 0, :, 0:3:2, :].bitcast(F32), ALU.subtract).then_inc(d_vl, 1)

            def maxima(k, s, pair):
                dve.wait_ge(e_s, 2 * k + pair + 1)
                after(dve, a_exp, 4 * k - 4)
                for q in (2 * pair, 2 * pair + 1):
                    ins = ve.tensor_reduce(negmax[:, s, q:q + 1], bS[q][:, :], AX_X, ALU.max, negate=True)
                ins.then_inc(d_max, 1)

            def inverse(k, s, pair):
                dve.wait_ge(a_exp, 4 * k + 2 * pair + 2)
                after(dve, g_pn, 4 * k - 4)
                ve.reciprocal(rinv[:, s, 2 * pair:2 * pair + 2], rsum[:, s, 2 * pair:2 * pair + 2]).then_inc(d_rinv, 1)

            def probs_lo(k, c):
                dve.wait_ge(a_pth, 4 * k + c + 1)
                ve.tensor_tensor(ptl[c][:, :], bT[c % 2][:, :], pth[c][:, :].bitcast(F32), ALU.subtract).then_inc(d_ptl, 1)

            def rows_out(t, half, par):
                dve.wait_ge(e_pv, 8 * t + 8)
                dve.wait_ge(ld_x2[par], 16 * (half + 1))
                ve.scalar_tensor_tensor(x2b[par][:, :], bO[:, :], gam[:, :], x2b[par][:, :], ALU.mult, ALU.add).then_inc(d_x2, 1)

            for t in range(2):
                first_norm(t, 0, t)
                aggregate(0, t)
                variance(0, t)
            dve.wait_ge(e_rg, 1)
            ve.tensor_copy(rgT[:, :, :], bM[:, 0:HC * NR].rearrange("p (c n) -> p c n", c=HC)).then_inc(d_rg, 1)
            values_lo(0, 0)
            maxima(0, 0, 0)
            maxima(0, 0, 1)
            inverse(0, 0, 0)
            inverse(0, 0, 1)
            maxima(1, 1, 0)

            def weights_lo(c):
                dve.wait_ge(a_wh, c + 1)
                ve.tensor_tensor(wsp[c][:, 1, :], stg[c % 2][:, :, :].rearrange("p a n -> p (a n)"),
                                 wsp[c][:, 0, :].bitcast(F32), ALU.subtract).then_inc(d_wl, 1)

            def tokens_lo(b, par):
                dve.wait_ge(a_xh, b + 1)
                v = xl[:, par, :, :, :]
                ve.tensor_tensor(v, v.bitcast(F32), xh[:, par, :, :, :].bitcast(F32), ALU.subtract).then_inc(d_xl, 1)

            def tile(t, i, par):
                k = 2 * t
                inverse(k + 1, 1, 0)
                maxima(k + 1, 1, 1)
                if there(t - 1):
                    rows_out(t - 1, i - 1 + par, 1 - par)
                probs_lo(k, 0)
                if there(t - 1):
                    dve.wait_ge(d_x2, t)
                    moments(1, t - 1, x2b[1 - par][:, :])
                probs_lo(k, 1)
                inverse(k + 1, 1, 1)
                if there(t - 1):
                    aggregate(1, t - 1)
                if there(t + 1):
                    maxima(k + 2, 0, 0)
                if there(t - 1):
                    variance(1, t - 1)
                probs_lo(k, 2)
                if there(t + 2):
                    first_norm(t + 2, i + 1, par)
                probs_lo(k, 3)
                if there(t + 2):
                    aggregate(0, t + 2)
                k = 2 * t + 1
                if there(t + 1):
                    inverse(k + 1, 0, 0)
                if there(t + 2):
                    variance(0, t + 2)
                if there(t + 1):
                    maxima(k + 1, 0, 1)
                probs_lo(k, 0)
                probs_lo(k, 1)
                if there(t + 1):
                    inverse(k + 1, 0, 1)
                    maxima(k + 2, 1, 0)
                probs_lo(k, 2)
                if there(t + 1):
                    values_lo(t + 1, 1 - par)
                probs_lo(k, 3)
                if isinstance(t, int) and t == NT - 1:
                    tokens_lo(0, 0)
                    weights_lo(0)
                    weights_lo(1)
            over_tiles(dve, tile)
            rows_out(NT - 1, NI - 1, 1)
            dve.wait_ge(d_x2, NT)
            moments(1, NT - 1, x2b[1][:, :])
            aggregate(1, NT - 1)
            variance(1, NT - 1)

            def hidden(b, c):
                n = SC * b + c
                p = c % 2
                dve.wait_ge(a_sg, n + 1)
                dve.wait_ge(e_u, n + 1)
                ve.tensor_tensor(sg[p][:, :], bU[p][:, :], sg[p][:, :], ALU.mult).then_inc(d_hm, 1)
                dve.wait_ge(a_hh, n + 1)
                ve.tensor_tensor(hl[p][:, :], sg[p][:, :], hh[p][:, :].bitcast(F32), ALU.subtract).then_inc(d_hl, 1)

            def outputs(b):
                dve.wait_ge(e_d, SC * (b + 1))
                for tt in range(TB):
                    n = TB * b + tt
                    dve.wait_ge(ld_xr[tt], 16 * (b + 1))
                    ve.scalar_tensor_tensor(xr[tt][:, :], bY[tt][:, :], sig[:, n:n + 1], xr[tt][:, :],
                                            ALU.mult, ALU.add).then_inc(d_out, 1)

            done = [0]

            def step_r(ins, wait=True):
                done[0] += 1
                ins.then_inc(d_r, 1)
                if wait:
                    dve.wait_ge(d_r, done[0])

            def bc(ap, shape):
                return ap.to_broadcast(shape)

            full = [P, NT, E]
            def less_maximum():
                dve.wait_ge(a_lg, NT)
                lgv = lg_all[:, :, 0:E]
                step_r(ve.tensor_reduce(nm[:, :], lgv, AX_X, ALU.max, negate=True))
                step_r(ve.tensor_tensor(ls[:, :, :], lgv, bc(nm[:, :].unsqueeze(2), full), ALU.add))
                assert done[0] == R_LS

            def probabilities():
                step_r(ve.tensor_copy(io8[:, :], io8i[:, :]))
                step_r(ve.tensor_copy(thr[:, :], thri[:, :]))
                step_r(ve.tensor_copy(sio[:, :], sioi[:, :]))
                dve.wait_ge(a_r, 2)
                step_r(ve.tensor_reduce(sm[:, :], ls[:, :, :], AX_X, ALU.add))
                step_r(ve.reciprocal(rc[:, :], sm[:, :]))
                step_r(ve.tensor_tensor(ls[:, :, :], ls[:, :, :], bc(rc[:, :].unsqueeze(2), full), ALU.mult))
                step_r(ve.tensor_scalar(ez[:, :], ez[:, :], 1.0, None, ALU.add))
                step_r(ve.reciprocal(sig[:, :], ez[:, :]))

            def two_largest():
                for t in range(NT):
                    step_r(ve.max(tv[:, t, :], ls[:, t, :]), False)
                dve.wait_ge(d_r, done[0])
                for t in range(NT):
                    step_r(ve.max_index(ti[:, t, :], tv[:, t, :], ls[:, t, :]), False)

            def one_hots():
                step_r(ve.tensor_tensor(sm[:, :], tv[:, :, 0], tv[:, :, 1], ALU.add))
                step_r(ve.reciprocal(rc[:, :], sm[:, :]))
                step_r(ve.tensor_tensor(msrc[:, :, :, 1].bitcast(F32), tv[:, :, 0:2], bc(rc[:, :].unsqueeze(2), [P, NT, 2]), ALU.mult))
                step_r(ve.tensor_copy(tif[:, :, :], ti[:, :, 0:2]))
                for k, m in enumerate((m1, m2)):
                    step_r(ve.tensor_tensor(m[:, :, :], bc(tif[:, :, k:k + 1], full), bc(io8[:, :].unsqueeze(1), full), ALU.is_equal))
                step_r(ve.tensor_tensor(ls[:, :, :], m1[:, :, :], m2[:, :, :], ALU.add))
                assert done[0] == R_M, done[0]

            def counts():
                dve.wait_ge(e_r, 1)
                step_r(ve.tensor_copy(pre_s[:, :, :], bY[0][:, 0:P].rearrange("p (t e) -> p t e", e=E)), False)
                step_r(ve.tensor_copy(tot_s[:, :, :], bY[0][:, P:2 * P].rearrange("p (t e) -> p t e", e=E)))
                assert done[0] == R_EV, done[0]

            def carries():
                step_r(ve.memset(carry[:, 0, :], 0.0))
                for t in range(1, NT):
                    step_r(ve.tensor_tensor(carry[:, t, :], carry[:, t - 1, :], tot_s[:, t - 1, :], ALU.add))
                step_r(ve.tensor_tensor(cnt[:, :], carry[:, NT - 1, :], tot_s[:, NT - 1, :], ALU.add))

            def slots():
                step_r(ve.tensor_tensor(cmpc[:, :, :], bc(cnt[:, :].unsqueeze(2), [P, E, 15]), bc(thr[:, :].unsqueeze(1), [P, E, 15]), ALU.is_gt))
                step_r(ve.tensor_reduce(nsl[:, :], cmpc[:, :, :], AX_X, ALU.add))
                step_r(ve.tensor_scalar(nsl[:, :], nsl[:, :], 1.0, None, ALU.add))
                step_r(ve.memset(sst[:, 0:1], 0.0))
                for e in range(1, E):
                    step_r(ve.tensor_tensor(sst[:, e:e + 1], sst[:, e - 1:e], nsl[:, e - 1:e], ALU.add))
                step_r(ve.tensor_tensor(scmp[:, :, :], bc(sio[:, :].unsqueeze(2), [1, 40, 7]), bc(sst[0:1, 1:E].unsqueeze(1), [1, 40, 7]), ALU.is_ge))
                step_r(ve.tensor_reduce(sexp[:, :], scmp[:, :, :], AX_X, ALU.add))
                step_r(ve.tensor_copy(slot_tab[:, :], sexp[:, :]))
                assert done[0] == R_TAB, done[0]

            def rows():
                step_r(ve.tensor_scalar(sst[:, :], sst[:, :], float(P), None, ALU.mult))
                step_r(ve.tensor_tensor(pre_s[:, :, :], pre_s[:, :, :], carry[:, :, :], ALU.add))
                step_r(ve.tensor_tensor(pre_s[:, :, :], pre_s[:, :, :], bc(sst[:, :].unsqueeze(1), full), ALU.add))
                for k, m in enumerate((m1, m2)):
                    step_r(ve.tensor_tensor(m[:, :, :], m[:, :, :], pre_s[:, :, :], ALU.mult))
                    step_r(ve.tensor_reduce(posf[:, :, k], m[:, :, :], AX_X, ALU.add))
                step_r(ve.tensor_copy(posi[:, :, :], posf[:, :, :]))
                assert done[0] == R_POS, done[0]

            beside = {(0, 0): less_maximum, (0, 2): probabilities, (0, 3): two_largest, (0, 4): one_hots,
                      (1, 1): carries, (1, 2): slots, (1, 3): rows}
            for b in range(NB):
                for c in range(SC):
                    if b == 1 and c == 1:
                        counts()
                    hidden(b, c)
                    if b == 0 and c + 2 < SC:
                        weights_lo(c + 2)
                    if c == 5 and b + 1 < NB:
                        tokens_lo(b + 1, (b + 1) % 2)
                    if c == 0 and b > 0:
                        outputs(b - 1)
                    if (b, c) in beside:
                        beside[b, c]()
            outputs(NB - 1)

            def hidden3(s, j):
                dve.wait_ge(a_sl, s + 1)
                dve.wait_ge(e_u3, s + 1)
                ve.tensor_tensor(h3[j % 2][:, :], bU3[j % 2][:, 0:I], h3[j % 2][:, :], ALU.mult).then_inc(d_h, 1)

            def hidden_T3(s, j):
                dve.wait_ge(e_th, s + 1)
                after(dve, e_d3, s - 1)
                ve.tensor_copy(hT3[j % 2][:, 0:IC - 1, :], bH3[:, 0:(IC - 1) * P].rearrange("p (c t) -> p c t", c=IC - 1)).then_inc(d_ht, 1)
                ve.tensor_copy(hT3[j % 2][0:IR, IC - 1, :], bH3[0:IR, (IC - 1) * P:IC * P]).then_inc(d_ht, 1)

            hidden3(0, 0)

            def slot(s, j):
                hidden_T3(s, j)
                if not (isinstance(s, int) and s + 1 >= SLOTS):
                    hidden3(s + 1, j + 1)
            over_slots(dve, slot)

        @block.tensor
        def _(pe):
            te = nc.tensor

            pe.wait_ge(ld_small, 48)
            pe.wait_ge(g_const, N_CONST)
            for c in range(HC):
                ins = te.transpose(bM[:, c * NR:(c + 1) * NR], rg[:, c * P:(c + 1) * P], ident[0:NR, 0:NR])
            ins.then_inc(e_rg, 1)

            def scores(k, t, par, s, pair):
                if pair == 0:
                    pe.wait_ge(g_ql, k + 1)
                    pe.wait_ge(g_kl, t + 1)
                after(pe, a_exp, 4 * k - 4 + 2 * pair + 2)
                for q in (2 * pair, 2 * pair + 1):
                    te.matmul(bS[q][:, :], qs[s][:, q * P:(q + 1) * P], kh[par][:, s, :], start=True, stop=False)
                    ins = te.matmul(bS[q][:, :], qs[s][:, q * P:(q + 1) * P], kl[par][:, s, :], start=False, stop=True)
                ins.then_inc(e_s, 1)

            def probs_T(k, s, c):
                if c == 0:
                    pe.wait_ge(g_pn, 4 * k + 4)
                after(pe, d_ptl, 4 * k + c - 1)
                for q in range(QC):
                    ins = te.transpose(bT[c % 2][:, q * P:(q + 1) * P], pb[s][:, q, c * P:(c + 1) * P], ident[:, :])
                ins.then_inc(e_t, 1)

            def times_v(k, t, s, par, c):
                if c == 0 and s == 0:
                    pe.wait_ge(d_vl, t + 1)
                    after(pe, d_x2, t)
                hi, lo = (vs[par][:, a, c, s:s + 2, :].rearrange("p a d -> p (a d)") for a in range(2))
                first, last = s == 0 and c == 0, s == 1 and c == LC - 1
                pe.wait_ge(a_pth, 4 * k + c + 1)
                te.matmul(bO[:, :], hi, pth[c][:, :], start=first, stop=False)
                te.matmul(bO[:, :], lo, pth[c][:, :], start=False, stop=False)
                pe.wait_ge(d_ptl, 4 * k + c + 1)
                te.matmul(bO[:, :], hi, ptl[c][:, :], start=False, stop=last).then_inc(e_pv, 1)

            def values_T(t, half, par):
                pe.wait_ge(ld_cn[par], 16 * (half + 1))
                if isinstance(t, int) and t < 2:
                    pe.wait_ge(d_rg, 1)
                if isinstance(t, int) and t == 2:
                    pe.wait_ge(d_vl, 2)
                after(pe, a_lg, t - 2)
                for c in range(LC):
                    ins = te.transpose(bM[:, c * P:(c + 1) * P], cn[par][:, c * P:(c + 1) * P], ident[:, :])
                ins.then_inc(e_vt, 1)

            def rows_T(t, par):
                pe.wait_ge(a_x2n, t + 1)
                if isinstance(t, int) and t + 2 >= NT:
                    pe.wait_ge(a_lg, t)
                else:
                    pe.wait_ge(d_vl, t + 3)
                for c in range(HC):
                    ins = te.transpose(bM[:, c * P:(c + 1) * P], x2n[par][:, c * P:(c + 1) * P], ident[:, :])
                ins.then_inc(e_x2T, 1)

            def logits(t, par):
                pe.wait_ge(a_x2T, t + 1)
                for c in range(HC):
                    ins = te.matmul(bM[:, 0:NR], x2T[par][:, c, :], rgT[:, c, :], start=(c == 0), stop=(c == HC - 1))
                ins.then_inc(e_lg, 1)

            values_T(0, 0, 0)
            scores(0, 0, 0, 0, 0)
            scores(0, 0, 0, 0, 1)
            scores(1, 0, 0, 1, 0)
            scores(1, 0, 0, 1, 1)

            def tile(t, i, par):
                k = 2 * t
                probs_T(k, 0, 0)
                probs_T(k, 0, 1)
                if there(t + 1):
                    scores(k + 2, t + 1, 1 - par, 0, 0)
                times_v(k, t, 0, par, 0)
                probs_T(k, 0, 2)
                times_v(k, t, 0, par, 1)
                probs_T(k, 0, 3)
                if there(t + 1):
                    scores(k + 2, t + 1, 1 - par, 0, 1)
                if there(t - 2):
                    logits(t - 2, par)
                times_v(k, t, 0, par, 2)
                times_v(k, t, 0, par, 3)
                k = 2 * t + 1
                probs_T(k, 1, 0)
                probs_T(k, 1, 1)
                if there(t + 1):
                    scores(k + 2, t + 1, 1 - par, 1, 0)
                times_v(k, t, 1, par, 0)
                if there(t + 1):
                    values_T(t + 1, i + par, 1 - par)
                probs_T(k, 1, 2)
                times_v(k, t, 1, par, 1)
                probs_T(k, 1, 3)
                if there(t + 1):
                    scores(k + 2, t + 1, 1 - par, 1, 1)
                times_v(k, t, 1, par, 2)
                if there(t - 1):
                    rows_T(t - 1, 1 - par)
                times_v(k, t, 1, par, 3)
            over_tiles(pe, tile)

            def gate_up(b, c, par):
                n = SC * b + c
                p = c % 2
                prev = n if c == 0 else n - 1
                if c == 0:
                    pe.wait_ge(d_xl, b + 1)
                if isinstance(b, int) and b == 0:
                    pe.wait_ge(d_wl, c + 1)
                w = wsp[c]
                for name, (bk, used, s_out) in enumerate(((bG[p], a_sg, e_g), (bU[p], d_hm, e_u))):
                    after(pe, used, prev)
                    for h in range(HC):
                        hi = w[:, 0, name * 512 + h * P:name * 512 + (h + 1) * P]
                        lo = w[:, 1, name * 512 + h * P:name * 512 + (h + 1) * P]
                        xhi, xlo = xh[:, par, :, h, :], xl[:, par, :, h, :]
                        te.matmul(bk[:, :], hi, xhi, start=(h == 0), stop=False)
                        te.matmul(bk[:, :], hi, xlo, start=False, stop=False)
                        ins = te.matmul(bk[:, :], lo, xhi, start=False, stop=(h == HC - 1))
                    ins.then_inc(s_out, 1)

            def down(b, c):
                n = SC * b + c
                p = c % 2
                pe.wait_ge(d_hl, n + 1)
                hi, lo = wsp[c][:, 0, 1024:1536], wsp[c][:, 1, 1024:1536]
                for tt in range(TB):
                    if c == 0:
                        after(pe, d_out, TB * b - TB + tt + 1)
                    th, tl = hh[p][:, tt * P:(tt + 1) * P], hl[p][:, tt * P:(tt + 1) * P]
                    te.matmul(bY[tt][:, :], th, hi, start=(c == 0), stop=False)
                    te.matmul(bY[tt][:, :], th, lo, start=False, stop=False)
                    ins = te.matmul(bY[tt][:, :], tl, hi, start=False, stop=(c == SC - 1))
                ins.then_inc(e_d, 1)

            def block2(b, par, last):
                for c in range(1, SC):
                    gate_up(b, c, par)
                    if b == 0 and c == 1:
                        pe.wait_ge(a_lg, NT)
                        pe.wait_ge(d_x2, NT)
                    if b == 1 and c == 1:
                        pe.wait_ge(d_r, R_M)
                        pe.wait_ge(d_out, 1)
                        te.matmul(bY[0][:, 0:P], tri[:, :], ls[:, :, :].rearrange("p t e -> p (t e)"), start=True, stop=True)
                        te.matmul(bY[0][:, P:2 * P], ones[:, :], ls[:, :, :].rearrange("p t e -> p (t e)"), start=True, stop=True).then_inc(e_r, 1)
                        pe.wait_ge(d_r, R_EV)
                    down(b, c - 1)
                if not last:
                    gate_up(b + 1, 0, 1 - par)
                down(b, SC - 1)

            logits(NT - 2, 0)
            gate_up(0, 0, 0)
            rows_T(NT - 1, 1)
            logits(NT - 1, 1)
            for b in range(NB):
                block2(b, b % 2, b == NB - 1)

            def rows3(s, turn, j):
                pe.wait_ge(ld_xg[j % 4], 16 * (turn + 1))
                after(pe, a_xt, s)
                for c in range(HC):
                    ins = te.transpose(bX3[:, c * P:(c + 1) * P], xg[j % 4][:, c * P:(c + 1) * P], ident[:, :])
                ins.then_inc(e_tx, 1)

            def expert_of(s):
                return te.value_load(slot_tab[0:1, s:s + 1] if isinstance(s, int) else slot_tab[0:1, bass.ds(s, 1)], min_val=0, max_val=E - 1)

            def gate_or_up(s, j, e, m):
                bk, used, done3 = ((bG3[j % 2], a_sl, e_g3), (bU3[j % 2], d_h, e_u3))[m]
                if m == 0:
                    if isinstance(s, int) and s < E:
                        pe.wait_ge(ld_ex[s], 64)
                    pe.wait_ge(a_xt, s + 1)
                after(pe, used, s - 1)
                for c in range(HC):
                    ins = te.matmul(bk[:, 0:I], xT3[j % 2][:, c, :], wex[:, e, (m * HC + c) * I:(m * HC + c + 1) * I],
                                    start=(c == 0), stop=(c == HC - 1))
                ins.then_inc(done3, 1)

            def hidden_T(s, j):
                pe.wait_ge(d_h, s + 1)
                after(pe, d_ht, 2 * s)
                for c in range(IC):
                    w = P if c < IC - 1 else IR
                    ins = te.transpose(bH3[0:w, c * P:(c + 1) * P], h3[j % 2][:, c * P:c * P + w], ident[:, :])
                ins.then_inc(e_th, 1)

            def down3(s, j, e):
                pe.wait_ge(d_ht, 2 * s + 2)
                after(pe, a_y, s - 1)
                for c in range(IC):
                    w = P if c < IC - 1 else IR
                    o = 2 * HC * I + c * H
                    ins = te.matmul(bY3[j % 2][:, :], hT3[j % 2][0:w, c, :], wex[0:w, e, o:o + H], start=(c == 0), stop=(c == IC - 1))
                ins.then_inc(e_d3, 1)

            pe.wait_ge(d_r, R_TAB)
            rows3(0, 0, 0)
            rows3(1, 0, 1)
            e0 = expert_of(0)
            gate_or_up(0, 0, e0, 0)
            gate_or_up(0, 0, e0, 1)
            pe.wait_ge(d_out, NT)

            def slot(s, turn, j):
                if not (isinstance(s, int) and s + 2 >= SLOTS):
                    rows3(s + 2, turn, j + 2)
                if isinstance(s, int) and s + 1 >= SLOTS:
                    hidden_T(s, j)
                else:
                    e = expert_of(s + 1)
                    gate_or_up(s + 1, j + 1, e, 0)
                    hidden_T(s, j)
                    gate_or_up(s + 1, j + 1, e, 1)
                down3(s, j, expert_of(s))

            for s in range(8):
                slot(s, (s + 2) // 4, s)
            with pe.Fori(2, SLOTS // 4) as i:
                for j in range(4):
                    slot(4 * i + j, i + (j + 2) // 4, j)
            for s in range(SLOTS // 4 * 4, SLOTS):
                slot(s, (s + 2) // 4, s)


def kernel(**inputs):
    import numpy as np
    import concourse.bacc as bacc
    from concourse.bass_utils import run_bass_kernel_spmd

    names = ["x", "ctx_2048", "L0_xattn_gamma", "L0_ffn_router_w", "L0_ffn_w_gate", "L0_ffn_w_up", "L0_ffn_w_down",
             "L0_ffn_sw_gate", "L0_ffn_sw_up", "L0_ffn_sw_down", "L0_ffn_shared_gate_w"]
    nc = bacc.Bacc("TRN2", target_bir_lowering=False, num_devices=1)
    arrays, args = {}, []
    for name in names:
        a = np.ascontiguousarray(inputs[name])
        if a.ndim == 0:
            a = a.reshape(1)
        arrays[f"in_{name}"] = a
        args.append(nc.dram_tensor(f"in_{name}", a.shape, mybir.dt.from_np(a.dtype), kind="ExternalInput").ap())
    shape = inputs["x"].shape
    rows = shape[0] * shape[1]
    args.append(nc.dram_tensor("out", (rows + P, shape[2]), F32, kind="ExternalOutput").ap())
    xattn_moe_kernel(nc, *args)
    r = run_bass_kernel_spmd(nc, [arrays], core_ids=[0])
    return r.results[0]["out"][:rows].reshape(shape)
```

```python
from contextlib import ExitStack

import concourse.bass as bass
from concourse import mybir

ALU = mybir.AluOpType
ACT = mybir.ActivationFunctionType
AX_X = mybir.AxisListType.X
F32 = mybir.dt.float32
F32R = mybir.dt.float32r
I32 = mybir.dt.int32
U32 = mybir.dt.uint32

P = 128
EPS = 1e-5


def xattn_moe_kernel(nc, x, ctx_in, gamma, router_w, w_gate, w_up, w_down, sw_gate, sw_up, sw_down, shared_gate_w, out):
    B, D, L = x.shape
    NH = 8
    DH = D // NH
    T = B * D
    H = L
    E, _, I = w_gate.shape
    SI = sw_gate.shape[1]
    NT = T // P
    HC = H // P
    LC = L // P
    QC = L // P
    NB = T // 512
    TB = 512 // P
    SC = SI // P
    IC = (I + P - 1) // P
    IR = I - (IC - 1) * P
    TOPK = 2
    SLOTS = (TOPK * T + (P - 1) * E) // P
    NR = E + 1
    NI = NT // 2
    NG = (SLOTS + 3) // 4
    assert DH == 64 and D == 512 and L == 512 and SI % P == 0 and NT % 2 == 0 and SLOTS == 39

    x_t = x.rearrange("b d l -> (b d) l").rearrange("(t p) l -> t p l", p=P)
    c_t = ctx_in.rearrange("b d l -> (b d) l").rearrange("(t p) l -> t p l", p=P)
    c_h = ctx_in.rearrange("b d l -> (b d) l").rearrange("(t s p) l -> t p s l", s=2, p=DH)
    x2_d = nc.dram_tensor("x2_rows", (T, H), F32, kind="Internal").ap()
    x2_t = x2_d.rearrange("(t p) h -> t p h", p=P)
    xn_d = nc.dram_tensor("x2_normed_rows", (T + P, H), F32, kind="Internal").ap()
    xT_d = nc.dram_tensor("x2_normed_transposed", (NT, P, H), F32, kind="Internal").ap()
    meta_d = nc.dram_tensor("slot_rows", (SLOTS * P, 2), I32, kind="Internal").ap()

    ctx = ExitStack()
    with ctx:
        def sem(name):
            return ctx.enter_context(nc.semaphore(name))

        def sems(name, n):
            return [sem(f"{name}{j}") for j in range(n)]

        base = (nc.sbuf_base + 31) // 32 * 32
        cursor = [base]

        def place(name, shape, dt=F32):
            n = 4
            for d in shape[1:]:
                n *= d
            t = nc.alloc_sbuf_tensor_at(name, list(shape), dt, offset=cursor[0])
            cursor[0] += (n + 31) // 32 * 32
            assert cursor[0] <= nc.sbuf_usable_end, (name, cursor[0])
            return t

        ident = place("ident", [P, P])
        tri = place("tri", [P, P])
        ones = place("ones", [P, P])
        rgT = place("rgT", [P, HC, NR])
        gam = place("gam", [P, 1])
        mhalf = place("mhalf", [P, 1])
        lg_all = place("lg_all", [P, NT, NR])
        sig = place("sig", [P, NT])
        posi = place("posi", [P, NT, TOPK], I32)
        msrc = place("msrc", [P, NT, TOPK, 2], I32)
        slot_tab = place("slot_tab", [1, NG], I32)
        meta = place("meta", [P, SLOTS, 2], I32)
        stats = place("stats", [P, 2, 6])
        aggr = place("aggr", [P, 2, 2])
        vare = place("vare", [P, 2, 1])
        rstd = place("rstd", [P, 2, 1])
        nmr = place("nmr", [P, 2, 1])
        negmax = place("negmax", [P, 2, QC])
        rsum = place("rsum", [P, 2, QC])
        rinv = place("rinv", [P, 2, QC])
        gidx = [place(f"gidx{j}", [P, 1], I32) for j in range(4)]
        sidx = [place(f"sidx{j}", [P, 1], I32) for j in range(4)]

        WCH = 3 * 512
        EW = 2 * HC * I + IC * H
        big = cursor[0]
        xb = [place(f"xb{j}", [P, L]) for j in range(2)]
        cn = [place(f"cn{j}", [P, L]) for j in range(2)]
        cd = [place(f"cd{j}", [P, 2, L]) for j in range(2)]
        kh = [place(f"kh{j}", [P, 2, L], F32R) for j in range(2)]
        kl = [place(f"kl{j}", [P, 2, L], F32R) for j in range(2)]
        xn = [place(f"xn{j}", [P, L]) for j in range(2)]
        qs = [place(f"qs{j}", [P, L], F32R) for j in range(2)]
        vs = [place(f"vs{j}", [P, 2, LC, 3, DH], F32R) for j in range(2)]
        pb = [place(f"pb{j}", [P, QC, L]) for j in range(2)]
        pth = [place(f"pth{j}", [P, L], F32R) for j in range(4)]
        ptl = [place(f"ptl{j}", [P, L], F32R) for j in range(4)]
        x2b = [place(f"x2b{j}", [P, L]) for j in range(2)]
        x2n = [place(f"x2n{j}", [P, H]) for j in range(2)]
        x2T = [place(f"x2T{j}", [P, HC, P]) for j in range(2)]
        rg = place("rg", [NR, H])
        zrow = place("zrow", [P, H])
        stage1_end = cursor[0]
        cursor[0] = big
        wsp = [place(f"wsp{c}", [P, 2, WCH], F32R) for c in range(SC)]
        cursor[0] = big
        wex = place("wex", [P, E, EW])
        big_end = cursor[0]
        assert stage1_end <= big_end
        stg0 = cursor[0]
        stg = [place(f"stg{j}", [P, 3, 512]) for j in range(2)]
        stg_end = cursor[0]
        x_hl = place("x_hl", [P, 2, 2, TB, HC, P], F32R)
        sg = [place(f"sg{j}", [P, 512]) for j in range(2)]
        hh = [place(f"hh{j}", [P, 512], F32R) for j in range(2)]
        hl = [place(f"hl{j}", [P, 512], F32R) for j in range(2)]
        xr = [place(f"xr{j}", [P, H]) for j in (0, 1)]
        tables0 = cursor[0]
        cursor[0] = stg0
        xr += [place(f"xr{j}", [P, H]) for j in (2, 3)]
        W3 = HC * I
        D3 = IC * H
        xg = [place(f"xg{j}", [P, H]) for j in range(2)]
        xT3 = [place(f"xT3{j}", [P, 2, HC, P], F32R) for j in range(2)]
        wg3 = place("wg3", [P, 2, W3], F32R)
        assert cursor[0] <= stg_end + 4 * 2 * TB * H
        wu3 = place("wu3", [P, 2, W3], F32R)
        h3 = [place(f"h3{j}", [P, IC * P]) for j in range(2)]
        hT3 = [place("hT30", [P, 2, IC, P], F32R)]
        assert cursor[0] <= stg_end + 2 * 4 * 2 * TB * H
        wd3 = place("wd3", [P, 2, D3], F32R)
        assert cursor[0] <= tables0 - 4 * 2 * H
        cursor[0] = tables0 - 4 * 2 * H
        y3 = [place(f"y3{j}", [P, H]) for j in range(2)]
        cursor[0] = stg0
        hT3.append(place("hT31", [P, 2, IC, P], F32R))
        cursor[0] = tables0
        ls = place("ls", [P, NT, E])
        pre_s = place("pre_s", [P, NT, E])
        tot_s = place("tot_s", [P, NT, E])
        carry = place("carry", [P, NT, E])
        m1 = place("m1", [P, NT, E])
        m2 = place("m2", [P, NT, E])
        tv = place("tv", [P, NT, 8])
        ti = place("ti", [P, NT, 8], U32)
        tif = place("tif", [P, NT, 2])
        io8 = place("io8", [P, E])
        io8i = place("io8i", [P, E], I32)
        thr = place("thr", [P, 15])
        thri = place("thri", [P, 15], I32)
        nm = place("nm", [P, NT])
        sm = place("sm", [P, NT])
        rc = place("rc", [P, NT])
        ez = place("ez", [P, NT])
        cnt = place("cnt", [P, E])
        cmpc = place("cmpc", [P, E, 15])
        nsl = place("nsl", [P, E])
        sst = place("sst", [P, E])
        posf = place("posf", [P, NT, 2])
        sio = place("sio", [1, 4 * NG + 4])
        sioi = place("sioi", [1, 4 * NG + 4], I32)
        scmp = place("scmp", [1, 4 * NG + 4, E - 1])
        sexp = place("sexp", [1, NG + 1, 4])
        packed = place("packed", [1, NG])

        bank = [ctx.enter_context(nc.psum_tensor(f"bank{j}", [P, 512], F32)) for j in range(8)]
        bS, bT, bO, bM = bank[0:4], bank[4:6], bank[6], bank[7]
        bG, bU, bY = bank[0:2], bank[2:4], bank[4:8]
        bX3, bG3, bU3, bH3, bY3 = bank[1], (bank[0], bank[4]), (bank[2], bank[5]), bank[3], bank[6:8]

        g_const, g_zero = sem("g_const"), sem("g_zero")
        ld_small = sem("ld_small")
        ld_x, ld_cn, ld_cd, ld_x2 = sems("ld_x", 2), sems("ld_cn", 2), sems("ld_cd", 2), sems("ld_x2", 2)
        e_rg, d_rg = sem("e_rg"), sem("d_rg")
        d_stat, d_aggr, d_vare = sems("d_stat", 2), sems("d_aggr", 2), sems("d_vare", 2)
        g_rstd, g_nmr, a_xn, g_kh, kl_done = sems("g_rstd", 2), sems("g_nmr", 2), sem("a_xn"), sem("g_kh"), sem("kl_done")
        a_qh, ql_done = sem("a_qh"), sem("ql_done")
        e_vt, a_vh, d_vl = sem("e_vt"), sem("a_vh"), sem("d_vl")
        e_s, d_max, a_exp, d_rinv, g_pn = sem("e_s"), sem("d_max"), sem("a_exp"), sem("d_rinv"), sem("g_pn")
        e_t, a_pth, d_ptl, e_pv = sem("e_t"), sem("a_pth"), sem("d_ptl"), sem("e_pv")
        d_x2 = sem("d_x2")
        a_x2n, e_x2T, a_x2T, e_lg, a_lg = sem("a_x2n"), sem("e_x2T"), sem("a_x2T"), sem("e_lg"), sem("a_lg")
        st_x2, st_x2n, st_x2T = sems("st_x2", 2), sems("st_x2n", 2), sems("st_x2T", 2)
        st_pad = sem("st_pad")
        ld_stg, ld_x2T, ld_xr, st_out = sems("ld_stg", 2), sems("ld_x2T", 2), sems("ld_xr", TB), sems("st_out", TB)
        a_wh, d_wl, a_xh, d_xl = sem("a_wh"), sem("d_wl"), sem("a_xh"), sem("d_xl")
        e_g, e_u, e_d = sem("e_g"), sem("e_u"), sem("e_d")
        a_sg, d_hm, a_hh, d_hl, d_out = sem("a_sg"), sem("d_hm"), sem("a_hh"), sem("d_hl"), sem("d_out")
        d_r, a_r, e_r = sem("d_r"), sem("a_r"), sem("e_r")
        st_meta0, st_meta = sem("st_meta0"), sem("st_meta")
        ld_ex = sems("ld_ex", E)
        ld_meta, ld_xg, st_y = sem("ld_meta"), sems("ld_xg", 2), sems("st_y", 2)
        g_gi, g_si = sem("g_gi"), sem("g_si")
        a_wg, d_wg, a_wu, d_wu, a_wd, d_wd, g_wd = sem("a_wg"), sem("d_wg"), sem("a_wu"), sem("d_wu"), sem("a_wd"), sem("d_wd"), sem("g_wd")
        e_tx, a_xt, d_xt, e_g3, e_u3, a_sl, d_h = sem("e_tx"), sem("a_xt"), sem("d_xt"), sem("e_g3"), sem("e_u3"), sem("a_sl"), sem("d_h")
        e_th, a_ht, d_ht, e_d3, a_y, d_hz = sem("e_th"), sem("a_ht"), sem("d_ht"), sem("e_d3"), sem("a_y"), sem("d_hz")

        N_CONST = 15
        R_LS = 2
        R_M = R_LS + 8 + 2 * NT + 7
        R_EV = R_M + 2
        R_TAB = R_EV + NT + 1 + 3 + E + 8
        R_POS = R_TAB + 3 + 2 * TOPK + 1

        def after(eng, s, value):
            if not isinstance(value, int) or value > 0:
                eng.wait_ge(s, value)

        def wait_ahead(eng, s, value):
            if isinstance(value, int):
                if value <= 0:
                    return
            else:
                eng.compute_val(value)
                eng.wait_ge(g_const, N_CONST)
            eng.wait_ge(s, value)

        def there(t):
            return not isinstance(t, int) or 0 <= t < NT

        def over_tiles(eng, tile):
            for i in (0, 1):
                for par in range(2):
                    tile(2 * i + par, i, par)
            with eng.Fori(2, NI - 1) as i:
                for par in range(2):
                    tile(2 * i + par, i, par)
            for par in range(2):
                tile(2 * (NI - 1) + par, NI - 1, par)

        def over_slots(eng, slot, reads_experts=False):
            def group(i, n):
                e = [None] * 5
                if reads_experts:
                    e = experts_from(eng, i)
                for j in range(n):
                    slot(4 * i + j, i, j, e[j], e[j + 1] if j < 4 else None)

            for i in range(2):
                group(i, 4)
            with eng.Fori(2, SLOTS // 4 - 1) as i:
                group(i, 4)
            group(SLOTS // 4 - 1, 4)
            group(SLOTS // 4, SLOTS % 4)

        def last_slots(s, ahead):
            return isinstance(s, int) and s + ahead >= SLOTS

        def experts_from(eng, i):
            at = slot_tab[0:1, i:i + 1] if isinstance(i, int) else slot_tab[0:1, bass.ds(i, 1)]
            word = eng.value_load(at, min_val=0, max_val=E ** 5 - 1)
            return [(word // E ** j) % E for j in range(5)]

        block = ctx.enter_context(nc.Block())

        @block.sync
        def _(sp):
            def load_x(t, par):
                after(sp, a_xn, t - 1)
                sp.dma_start(xb[par][:, :], x_t[t, :, :]).then_inc(ld_x[par], 16)

            def load_keys(t, par):
                after(sp, kl_done, t - 1)
                for half in range(2):
                    sp.dma_start(cd[par][DH * half:DH * (half + 1), :, :], c_h[t, :, :, :]).then_inc(ld_cd[par], 16)

            def load_values(t, par):
                after(sp, e_vt, t - 1)
                sp.dma_start(cn[par][:, :], c_t[t, :, :]).then_inc(ld_cn[par], 16)

            def load_x2(t, half, par):
                if not isinstance(t, int):
                    sp.compute_val(16 * half)
                after(sp, a_x2n, t - 1)
                after(sp, st_x2[par], 16 * half)
                sp.dma_start(x2b[par][:, :], x_t[t, :, :]).then_inc(ld_x2[par], 16)

            def store_rows(t, par):
                sp.wait_ge(d_x2, t + 1)
                sp.dma_start(x2_t[t, :, :], x2b[par][:, :]).then_inc(st_x2[par], 16)
                sp.wait_ge(a_x2n, t + 1)
                sp.dma_start(xn_d[0:T, :].rearrange("(t p) h -> t p h", p=P)[t, :, :], x2n[par][:, :]).then_inc(st_x2n[par], 16)

            def store_columns(t, par):
                sp.wait_ge(a_x2T, t + 1)
                sp.dma_start(xT_d[t, :, :], x2T[par][:, :, :].rearrange("p c t -> p (c t)")).then_inc(st_x2T[par], 16)

            load_x(0, 0)
            load_keys(0, 0)
            load_values(0, 0)
            load_x(1, 1)
            load_keys(1, 1)
            load_values(1, 1)
            sp.dma_start(gam[:, :], gamma.partition_broadcast(P)).then_inc(ld_small, 16)
            sp.dma_start(rg[0:E, :], router_w).then_inc(ld_small, 16)
            sp.dma_start(rg[E:NR, :], shared_gate_w.rearrange("(a h) -> a h", a=1)).then_inc(ld_small, 16)
            load_x2(0, 0, 0)
            sp.wait_ge(g_zero, 1)
            sp.dma_start(out[T:T + P, :], zrow[:, :]).then_inc(st_pad, 16)
            sp.dma_start(xn_d[T:T + P, :], zrow[:, :]).then_inc(st_pad, 16)
            sp.wait_ge(g_const, N_CONST)
            sp.dma_start(meta_d.rearrange("(s p) c -> p s c", p=P), meta[:, :, :]).then_inc(st_meta0, 16)

            g_c = sw_gate.rearrange("(h p) (c n) -> c p h n", p=P, n=P)
            u_c = sw_up.rearrange("(h p) (c n) -> c p h n", p=P, n=P)
            d_c = sw_down.rearrange("(c p) n -> c p n", p=P)

            def load_chunk(c):
                after(sp, d_wl, c - 1)
                for n, src in enumerate((g_c[c, :, :, :], u_c[c, :, :, :])):
                    sp.dma_start(stg[c % 2][:, n, :].rearrange("p (h n) -> p h n", h=HC), src).then_inc(ld_stg[c % 2], 16)
                sp.dma_start(stg[c % 2][:, 2, :], d_c[c, :, :]).then_inc(ld_stg[c % 2], 16)

            def load_block(b, par):
                for q in range(2):
                    sp.wait_ge(st_x2T[q], 16 * (TB * (b + 1) // 2))
                after(sp, e_u, SC * (b - 1))
                sp.dma_start(x_hl[:, par, 1, :, :, :].bitcast(F32).rearrange("p t c n -> p t (c n)"),
                             xT_d.rearrange("(b t) p n -> b p t n", t=TB)[b, :, :, :]).then_inc(ld_x2T[par], 16)

            def tile(t, i, par):
                if isinstance(t, int) and t == NT - 2:
                    load_chunk(0)
                    load_chunk(1)
                    load_block(0, 0)
                    load_block(1, 1)
                if there(t + 2):
                    load_x(t + 2, par)
                    load_keys(t + 2, par)
                if there(t - 2):
                    store_columns(t - 2, par)
                if there(t - 1):
                    store_rows(t - 1, 1 - par)
                if there(t + 1):
                    load_x2(t + 1, i + par, 1 - par)
                if there(t + 2):
                    load_values(t + 2, par)
            over_tiles(sp, tile)

            store_columns(NT - 2, 0)
            store_rows(NT - 1, 1)
            store_columns(NT - 1, 1)
            for c in range(2, SC):
                load_chunk(c)

            def load_rows(b):
                for tt in range(TB):
                    after(sp, st_out[tt], 16 * b)
                    sp.dma_start(xr[tt][:, :], x2_t[TB * b + tt, :, :]).then_inc(ld_xr[tt], 16)

            def store_out(b):
                for tt in range(TB):
                    n = TB * b + tt
                    sp.wait_ge(d_out, n + 1)
                    sp.dma_start(out[0:T, :].rearrange("(t p) h -> t p h", p=P)[n, :, :], xr[tt][:, :]).then_inc(st_out[tt], 16)

            for q in range(2):
                sp.wait_ge(st_x2[q], 16 * NI)
            sp.wait_ge(d_wl, SC)
            load_rows(0)
            load_block(2, 0)
            store_out(0)
            load_rows(1)
            load_block(3, 1)
            store_out(1)
            load_rows(2)
            sp.wait_ge(st_meta, 16 * NT * TOPK)
            sp.dma_start(meta[:, :, :], meta_d.rearrange("(s p) c -> p s c", p=P)).then_inc(ld_meta, 16)
            store_out(2)
            load_rows(3)

            def load_expert(e):
                under = min(SC - 1, (EW * (e + 1) - 1) // (2 * WCH))
                sp.wait_ge(e_d, SC * (NB - 1) + under + 1)
                w = wex[:, e, :]
                sp.dma_start(w[:, 0:HC * I].rearrange("p (c i) -> p c i", c=HC),
                             w_gate[e, :, :].rearrange("(c p) i -> p c i", p=P)).then_inc(ld_ex[e], 16)
                sp.dma_start(w[:, HC * I:2 * HC * I].rearrange("p (c i) -> p c i", c=HC),
                             w_up[e, :, :].rearrange("(c p) i -> p c i", p=P)).then_inc(ld_ex[e], 16)
                sp.dma_start(w[:, 2 * HC * I:2 * HC * I + (IC - 1) * H].rearrange("p (c h) -> p c h", c=IC - 1),
                             w_down[e, 0:(IC - 1) * P, :].rearrange("(c p) h -> p c h", p=P)).then_inc(ld_ex[e], 16)
                sp.dma_start(w[0:IR, 2 * HC * I + (IC - 1) * H:EW], w_down[e, (IC - 1) * P:I, :]).then_inc(ld_ex[e], 16)

            for e in range(E):
                if e == E - 3:
                    store_out(NB - 1)
                load_expert(e)
            sp.wait_ge(st_y[0], 16 * ((SLOTS + 1) // 2))
            sp.wait_ge(st_y[1], 16 * (SLOTS // 2))
            for tt in range(TB):
                sp.wait_ge(st_out[tt], 16 * NB)
            for q in range(2):
                sp.wait_ge(st_x2[q], 16 * NI)
                sp.wait_ge(st_x2n[q], 16 * NI)
                sp.wait_ge(st_x2T[q], 16 * NI)
            sp.wait_ge(st_pad, 32)
            sp.wait_ge(st_meta0, 16)

        @block.gpsimd
        def _(g):
            gp = nc.gpsimd
            made = [0]

            def const(ins):
                made[0] += 1
                ins.then_inc(g_const, 1)

            const(gp.memset(ident[:, :], 0.0))
            const(gp.memset(tri[:, :], 1.0))
            const(gp.memset(ones[:, :], 1.0))
            const(gp.memset(mhalf[:, :], -0.5))
            for par in range(2):
                const(gp.memset(vs[par][:, :, :, 1, :].bitcast(F32), 0.0))
            g.wait_ge(g_const, 6)
            const(gp.affine_select(out=ident[:, :], in_=ident[:, :], compare_op=ALU.not_equal, fill=1.0,
                                   base=0, pattern=[[-1, P]], channel_multiplier=1))
            const(gp.affine_select(out=tri[:, :], in_=tri[:, :], compare_op=ALU.is_gt, fill=0.0,
                                   base=0, pattern=[[1, P]], channel_multiplier=-1))
            const(gp.iota(meta[:, :, 0], pattern=[[0, SLOTS]], base=T, channel_multiplier=1))
            const(gp.memset(meta[:, :, 1], 0))
            for k in range(TOPK):
                const(gp.iota(msrc[:, :, k, 0], pattern=[[P, NT]], base=0, channel_multiplier=1))
            const(gp.iota(io8i[:, :], pattern=[[1, E]], base=0, channel_multiplier=0))
            const(gp.iota(thri[:, :], pattern=[[P, 15]], base=P, channel_multiplier=0))
            const(gp.iota(sioi[:, :], pattern=[[1, 4 * NG + 4]], base=0, channel_multiplier=0))
            assert made[0] == N_CONST

            gp.memset(zrow[:, :], 0.0).then_inc(g_zero, 1)

            def power(kind, n):
                after(g, (a_xn, a_x2n)[kind], n)
                g.wait_ge(d_vare[kind], n + 1)
                gp.tensor_tensor(rstd[:, kind, :], vare[:, kind, :], mhalf[:, :], ALU.pow).then_inc(g_rstd[kind], 1)
                wait_ahead(g, g_rstd[kind], n + 1)
                gp.tensor_scalar(nmr[:, kind, :], aggr[:, kind, 0:1], rstd[:, kind, :], -1.0, ALU.mult, ALU.mult).then_inc(g_nmr[kind], 1)

            def queries_lo(t, s, par, before, count):
                g.wait_ge(before, count)
                g.wait_ge(a_qh, 2 * t + s + 1)
                r = slice(DH * s, DH * (s + 1))
                o = slice(DH * (1 - s), DH * (2 - s))
                gp.tensor_tensor(qs[s][o, :], xn[par][r, :], qs[s][r, :].bitcast(F32), ALU.subtract).then_inc(ql_done, 1)
                wait_ahead(g, ql_done, 2 * t + s + 1)

            def keys_hi(t, half, par):
                wait_ahead(g, e_s, 8 * t - 8)
                wait_ahead(g, ld_cd[par], 32 * (half + 1))
                gp.tensor_scalar(kh[par][:, :, :], cd[par][:, :, :], 1.0, 0.0, ALU.mult, ALU.add).then_inc(g_kh, 1)

            def keys_lo(t, par):
                g.wait_ge(g_kh, t + 1)
                gp.tensor_tensor(kl[par][:, :, :], cd[par][:, :, :], kh[par][:, :, :].bitcast(F32), ALU.subtract).then_inc(kl_done, 1)

            def norm_p(k, s, pair):
                wait_ahead(g, d_rinv, 2 * k + pair + 1)
                for q in (2 * pair, 2 * pair + 1):
                    gp.tensor_scalar(pb[s][:, q, :], pb[s][:, q, :], rinv[:, s, q:q + 1], 0.0,
                                     ALU.mult, ALU.add).then_inc(g_pn, 1)

            g.wait_ge(g_const, N_CONST)
            power(0, 0)
            power(0, 1)
            keys_hi(1, 0, 1)
            keys_lo(1, 1)
            norm_p(0, 0, 0)
            queries_lo(1, 0, 1, g_pn, 2)
            norm_p(0, 0, 1)

            def tile(t, i, par):
                k = 2 * t
                norm_p(k + 1, 1, 0)
                if there(t + 2):
                    keys_hi(t + 2, i + 1, par)
                norm_p(k + 1, 1, 1)
                if there(t - 1):
                    power(1, t - 1)
                if there(t + 1):
                    if there(t - 1):
                        queries_lo(t + 1, 1, 1 - par, g_nmr[1], t)
                    else:
                        queries_lo(t + 1, 1, 1 - par, g_pn, 4 * k + 8)
                if there(t + 2):
                    power(0, t + 2)
                if there(t + 1):
                    norm_p(k + 2, 0, 0)
                if there(t + 2):
                    keys_lo(t + 2, par)
                if there(t + 1):
                    norm_p(k + 2, 0, 1)
                if there(t + 2):
                    queries_lo(t + 2, 0, par, g_pn, 4 * k + 12)
            over_tiles(g, tile)
            power(1, NT - 1)

            g.wait_ge(d_r, R_POS)
            g.wait_ge(st_meta0, 16)
            for t in range(NT):
                for k in range(TOPK):
                    g.indirect_dma_start(out=meta_d, out_offset=bass.IndirectOffsetOnAxis(ap=posi[:, t, k:k + 1], axis=0),
                                         in_=msrc[:, t, k, :], in_offset=None).then_inc(st_meta, 16)
            g.wait_ge(st_x2n[0], 16 * NI)
            g.wait_ge(st_x2n[1], 16 * NI)
            g.wait_ge(st_pad, 32)
            g.wait_ge(ld_meta, 16)
            g.wait_ge(d_wl, SC)

            def gather(s, half, j):
                if not isinstance(s, int) or s >= 4:
                    wait_ahead(g, ld_xg[j % 2], 16 * (half - 1))
                gp.tensor_copy(gidx[j % 4][:, :], meta[:, s, 0:1]).then_inc(g_gi, 1)
                wait_ahead(g, e_tx, s - 1)
                wait_ahead(g, g_gi, s + 1)
                g.indirect_dma_start(out=xg[j % 2][:, :], out_offset=None, in_=xn_d,
                                     in_offset=bass.IndirectOffsetOnAxis(ap=gidx[j % 4][:, 0:1], axis=0)).then_inc(ld_xg[j % 2], 16)

            def scatter(s, half, j):
                gp.tensor_copy(sidx[j % 4][:, :], meta[:, s, 0:1]).then_inc(g_si, 1)
                if isinstance(s, int) and s == 0:
                    for tt in range(TB):
                        g.wait_ge(st_out[tt], 16 * NB)
                else:
                    wait_ahead(g, st_y[(j + 1) % 2], 16 * half)
                wait_ahead(g, a_y, s + 1)
                wait_ahead(g, g_si, s + 1)
                g.indirect_dma_start(out=out, out_offset=bass.IndirectOffsetOnAxis(ap=sidx[j % 4][:, 0:1], axis=0),
                                     in_=y3[j % 2][:, :], in_offset=None, compute_op=ALU.add).then_inc(st_y[j % 2], 16)

            def down_lo(s, e):
                wait_ahead(g, a_wd, s + 1)
                c = slice((IC - 1) * H, IC * H)
                gp.tensor_tensor(wd3[0:IR, 1, c], wex[0:IR, e, 2 * W3 + (IC - 1) * H:EW], wd3[0:IR, 0, c].bitcast(F32), ALU.subtract).then_inc(g_wd, 1)

            for s in range(4):
                gather(s, s // 2, s)
            g.wait_ge(d_r, R_TAB)
            down_lo(0, 0)

            def slot(s, i, j, e1, e2):
                if not last_slots(s, 4):
                    gather(s + 4, 2 * i + 2 + j // 2, j)
                if not last_slots(s, 1):
                    down_lo(s + 1, e1)
                scatter(s, 2 * i + (j + 1) // 2, j)
            over_slots(g, slot, reads_experts=True)

        @block.scalar
        def _(act):
            sc = nc.scalar

            def normed(kind, t, half, par):
                act.wait_ge(g_nmr[kind], t + 1)
                if kind == 0:
                    after(act, ql_done, 2 * t - 2)
                    sc.activation(xn[par][:, :], xb[par][:, :], ACT.Identity, bias=nmr[:, 0, :], scale=rstd[:, 0, :]).then_inc(a_xn, 1)
                else:
                    after(act, st_x2n[par], 16 * half)
                    after(act, e_x2T, t - 1)
                    sc.activation(x2n[par][:, :], x2b[par][:, :], ACT.Identity, bias=nmr[:, 1, :], scale=rstd[:, 1, :]).then_inc(a_x2n, 1)

            def queries_hi(t, s, par):
                act.wait_ge(a_xn, t + 1)
                after(act, e_s, 4 * (2 * t - 2 + s) + 4)
                r = slice(DH * s, DH * (s + 1))
                sc.activation(qs[s][r, :], xn[par][r, :], ACT.Copy).then_inc(a_qh, 1)

            def values_hi(t, par):
                act.wait_ge(e_vt, t + 1)
                after(act, e_pv, 8 * t - 8)
                sc.activation(vs[par][:, 0, :, 0:3:2, :], bM[:, :].rearrange("p (c s d) -> p c s d", c=LC, s=2),
                              ACT.Copy).then_inc(a_vh, 1)

            def exps(k, s, pair):
                after(act, e_t, 4 * k - 4)
                after(act, g_pn, 4 * k - 4)
                for q in (2 * pair, 2 * pair + 1):
                    act.wait_ge(d_max, 4 * k + q + 1)
                    sc.activation(pb[s][:, q, :], bS[q][:, :], ACT.Exp, bias=negmax[:, s, q:q + 1], scale=1.0,
                                  accum_out=rsum[:, s, q:q + 1]).then_inc(a_exp, 1)

            def probs_hi(k, c):
                act.wait_ge(e_t, 4 * k + c + 1)
                after(act, e_pv, 4 * k + c - 3)
                sc.activation(pth[c][:, :], bT[c % 2][:, :], ACT.Copy).then_inc(a_pth, 1)

            def rows_T(t, half, par):
                act.wait_ge(e_x2T, t + 1)
                after(act, st_x2T[par], 16 * half)
                after(act, e_lg, t - 1)
                sc.activation(x2T[par][:, :, :], bM[:, :].rearrange("p (c t) -> p c t", c=HC), ACT.Copy).then_inc(a_x2T, 1)

            def logits(t):
                act.wait_ge(e_lg, t + 1)
                sc.activation(lg_all[:, t, :], bM[:, 0:NR], ACT.Copy).then_inc(a_lg, 1)

            normed(0, 0, 0, 0)
            queries_hi(0, 0, 0)
            queries_hi(0, 1, 0)
            values_hi(0, 0)
            normed(0, 1, 0, 1)
            exps(0, 0, 0)
            exps(0, 0, 1)
            queries_hi(1, 0, 1)
            exps(1, 1, 0)

            def weights_hi(c):
                act.wait_ge(ld_stg[c % 2], 48 * (c // 2 + 1))
                sc.activation(wsp[c][:, 0, :], stg[c % 2][:, :, :].rearrange("p a n -> p (a n)"), ACT.Copy).then_inc(a_wh, 1)

            def tokens_hi(b, par):
                act.wait_ge(ld_x2T[par], 16 * (b // 2 + 1) if isinstance(b, int) else 16)
                after(act, e_u, SC * (b - 1))
                sc.activation(x_hl[:, par, 0, :, :, :], x_hl[:, par, 1, :, :, :].bitcast(F32), ACT.Copy).then_inc(a_xh, 1)

            def tile(t, i, par):
                k = 2 * t
                probs_hi(k, 0)
                probs_hi(k, 1)
                exps(k + 1, 1, 1)
                if there(t - 2):
                    rows_T(t - 2, i - 1, par)
                if there(t + 1):
                    queries_hi(t + 1, 1, 1 - par)
                probs_hi(k, 2)
                probs_hi(k, 3)
                if not there(t + 1):
                    tokens_hi(0, 0)
                if there(t + 1):
                    exps(k + 2, 0, 0)
                if there(t - 2):
                    logits(t - 2)
                k = 2 * t + 1
                probs_hi(k, 0)
                probs_hi(k, 1)
                if not there(t + 1):
                    act.wait_ge(a_xn, NT)
                    act.wait_ge(e_vt, NT)
                    act.wait_ge(kl_done, NT)
                    weights_hi(0)
                if there(t + 1):
                    exps(k + 1, 0, 1)
                if there(t - 1):
                    normed(1, t - 1, i - 1 + par, 1 - par)
                probs_hi(k, 2)
                if there(t + 1):
                    values_hi(t + 1, 1 - par)
                probs_hi(k, 3)
                if there(t + 2):
                    normed(0, t + 2, i + 1, par)
                if there(t + 1):
                    exps(k + 2, 1, 0)
                if there(t + 2):
                    queries_hi(t + 2, 0, par)
                if not there(t + 1):
                    act.wait_ge(e_s, 8 * NT)
                    weights_hi(1)
            over_tiles(act, tile)
            rows_T(NT - 2, NI - 1, 0)
            logits(NT - 2)
            normed(1, NT - 1, NI - 1, 1)
            rows_T(NT - 1, NI - 1, 1)
            logits(NT - 1)

            act.wait_ge(e_lg, NT)
            act.wait_ge(a_x2n, NT)
            act.wait_ge(a_lg, NT)
            act.wait_ge(d_x2, NT)
            for q in range(2):
                act.wait_ge(st_x2[q], 16 * NI)
                act.wait_ge(st_x2n[q], 16 * NI)
                act.wait_ge(st_x2T[q], 16 * NI)
            act.wait_ge(st_pad, 32)

            def silu_hi(b, c):
                n = SC * b + c
                p = c % 2
                act.wait_ge(e_g, n + 1)
                prev = n if c == 0 else n - 1
                after(act, d_hl, prev)
                sc.activation(sg[p][:, :], bG[p][:, :], ACT.Silu).then_inc(a_sg, 1)

            def hidden_hi(b, c):
                n = SC * b + c
                p = c % 2
                act.wait_ge(d_hm, n + 1)
                after(act, e_d, n if c == 0 else n - 1)
                sc.activation(hh[p][:, :], sg[p][:, :], ACT.Copy).then_inc(a_hh, 1)

            for c in range(SC):
                silu_hi(0, c)
                if c + 2 < SC:
                    weights_hi(c + 2)
                if c == 5:
                    tokens_hi(1, 1)
                hidden_hi(0, c)
                if c == 1:
                    act.wait_ge(d_r, R_LS)
                    sc.activation(ls[:, :, :], ls[:, :, :], ACT.Exp).then_inc(a_r, 1)
                    sc.activation(ez[:, :], lg_all[:, :, E], ACT.Exp, scale=-1.0).then_inc(a_r, 1)
            def gate_hi(s, e):
                if isinstance(s, int) and s < E:
                    act.wait_ge(ld_ex[s], 64)
                wait_ahead(act, e_g3, s)
                sc.activation(wg3[:, 0, :], wex[:, e, 0:W3], ACT.Copy).then_inc(a_wg, 1)

            def up_hi(s, e):
                wait_ahead(act, e_u3, s)
                sc.activation(wu3[:, 0, :], wex[:, e, W3:2 * W3], ACT.Copy).then_inc(a_wu, 1)

            for b in range(1, NB):
                for c in range(SC):
                    silu_hi(b, c)
                    if b == NB - 1 and c == SC - 3:
                        act.wait_ge(e_u, SC * (NB - 1))
                        act.wait_ge(d_r, R_TAB)
                        gate_hi(0, 0)
                    if c == 5 and b + 1 < NB:
                        tokens_hi(b + 1, (b + 1) % 2)
                    hidden_hi(b, c)

            def rows_hi(s, j):
                act.wait_ge(e_tx, s + 1)
                wait_ahead(act, e_u3, s - 1)
                sc.activation(xT3[j % 2][:, 0, :, :], bX3[:, :].rearrange("p (c t) -> p c t", c=HC), ACT.Copy).then_inc(a_xt, 1)

            def silu3(s, j):
                wait_ahead(act, e_g3, s + 1)
                wait_ahead(act, e_th, s - 1)
                sc.activation(h3[j % 2][:, 0:I], bG3[j % 2][:, 0:I], ACT.Silu).then_inc(a_sl, 1)

            def hidden_T_hi(s, j):
                wait_ahead(act, e_th, s + 1)
                wait_ahead(act, e_d3, s - 1)
                sc.activation(hT3[j % 2][:, 0, :, :], bH3[:, 0:IC * P].rearrange("p (c t) -> p c t", c=IC), ACT.Copy).then_inc(a_ht, 1)

            def down_hi(s, e):
                wait_ahead(act, e_d3, s)
                sc.activation(wd3[:, 0, 0:2 * H], wex[:, e, 2 * W3:2 * W3 + 2 * H], ACT.Copy)
                sc.activation(wd3[0:IR, 0, 2 * H:D3], wex[0:IR, e, 2 * W3 + 2 * H:EW], ACT.Copy).then_inc(a_wd, 1)

            def weigh(s, half, j):
                wait_ahead(act, e_d3, s + 1)
                wait_ahead(act, st_y[j % 2], 16 * half)
                sc.activation(y3[j % 2][:, :], bY3[j % 2][:, :], ACT.Copy,
                              scale=meta[:, s, 1:2].bitcast(F32)).then_inc(a_y, 1)

            act.wait_ge(e_u, SC * NB)
            rows_hi(0, 0)
            up_hi(0, 0)
            e1 = experts_from(act, 0)[0]
            act.wait_ge(e_d, SC * NB)
            down_hi(0, 0)
            rows_hi(1, 1)
            silu3(0, 0)
            gate_hi(1, e1)
            up_hi(1, e1)

            def slot(s, i, j, e1, e2):
                if not last_slots(s, 2):
                    rows_hi(s + 2, j + 2)
                if not last_slots(s, 1):
                    silu3(s + 1, j + 1)
                if isinstance(s, int) and s == 1:
                    for tt in range(2, TB):
                        act.wait_ge(st_out[tt], 16 * NB)
                hidden_T_hi(s, j)
                if not last_slots(s, 2):
                    gate_hi(s + 2, e2)
                    up_hi(s + 2, e2)
                if isinstance(s, int) and s == 0:
                    for tt in range(2):
                        act.wait_ge(st_out[tt], 16 * NB)
                if not last_slots(s, 1):
                    down_hi(s + 1, e1)
                weigh(s, 2 * i + j // 2, j)
            over_slots(act, slot, reads_experts=True)

        @block.vector
        def _(dve):
            ve = nc.vector

            def moments(kind, n, src):
                ve.bn_stats(stats[:, kind, :], src).then_inc(d_stat[kind], 1)

            def aggregate(kind, n):
                wait_ahead(dve, g_nmr[kind], n)
                wait_ahead(dve, d_stat[kind], n + 1)
                ve.bn_aggr(aggr[:, kind, :], stats[:, kind, :]).then_inc(d_aggr[kind], 1)

            def variance(kind, n):
                dve.wait_ge(d_aggr[kind], n + 1)
                scale = (float(DH), 1.0)[kind]
                ve.tensor_scalar(vare[:, kind, :], aggr[:, kind, 1:2], scale, scale * EPS, ALU.mult, ALU.add).then_inc(d_vare[kind], 1)

            def first_norm(t, half, par):
                dve.wait_ge(ld_x[par], 16 * (half + 1))
                moments(0, t, xb[par][:, :])

            def values_lo(t, par):
                dve.wait_ge(a_vh, t + 1)
                ve.tensor_tensor(vs[par][:, 1, :, 0:3:2, :], bM[:, :].rearrange("p (c s d) -> p c s d", c=LC, s=2),
                                 vs[par][:, 0, :, 0:3:2, :].bitcast(F32), ALU.subtract).then_inc(d_vl, 1)

            def maxima(k, s, pair):
                after(dve, a_exp, 4 * k - 4)
                for q in (2 * pair, 2 * pair + 1):
                    dve.wait_ge(e_s, 4 * k + q + 1)
                    ve.tensor_reduce(negmax[:, s, q:q + 1], bS[q][:, :], AX_X, ALU.max, negate=True).then_inc(d_max, 1)

            def inverse(k, s, pair):
                dve.wait_ge(a_exp, 4 * k + 2 * pair + 2)
                after(dve, g_pn, 4 * k - 4)
                ve.reciprocal(rinv[:, s, 2 * pair:2 * pair + 2], rsum[:, s, 2 * pair:2 * pair + 2]).then_inc(d_rinv, 1)

            def probs_lo(k, c):
                dve.wait_ge(a_pth, 4 * k + c + 1)
                ve.tensor_tensor(ptl[c][:, :], bT[c % 2][:, :], pth[c][:, :].bitcast(F32), ALU.subtract).then_inc(d_ptl, 1)

            def rows_out(t, half, par):
                dve.wait_ge(e_pv, 8 * t + 8)
                dve.wait_ge(ld_x2[par], 16 * (half + 1))
                ve.scalar_tensor_tensor(x2b[par][:, :], bO[:, :], gam[:, :], x2b[par][:, :], ALU.mult, ALU.add).then_inc(d_x2, 1)

            first_norm(0, 0, 0)
            aggregate(0, 0)
            variance(0, 0)
            dve.wait_ge(ld_cd[0], 32)
            ve.tensor_copy(kh[0][:, :, :], cd[0][:, :, :]).then_inc(g_kh, 1)
            first_norm(1, 0, 1)
            dve.wait_ge(g_kh, 1)
            ve.tensor_tensor(kl[0][:, :, :], cd[0][:, :, :], kh[0][:, :, :].bitcast(F32), ALU.subtract).then_inc(kl_done, 1)
            for s in range(2):
                dve.wait_ge(a_qh, s + 1)
                r, o = slice(DH * s, DH * (s + 1)), slice(DH * (1 - s), DH * (2 - s))
                ve.tensor_tensor(qs[s][o, :], xn[0][r, :], qs[s][r, :].bitcast(F32), ALU.subtract).then_inc(ql_done, 1)
            aggregate(0, 1)
            variance(0, 1)
            values_lo(0, 0)
            maxima(0, 0, 0)
            maxima(0, 0, 1)
            inverse(0, 0, 0)
            inverse(0, 0, 1)
            maxima(1, 1, 0)
            dve.wait_ge(e_rg, 1)
            ve.tensor_copy(rgT[:, :, :], bO[:, 0:HC * NR].rearrange("p (c n) -> p c n", c=HC)).then_inc(d_rg, 1)

            def weights_lo(c):
                dve.wait_ge(a_wh, c + 1)
                ve.tensor_tensor(wsp[c][:, 1, :], stg[c % 2][:, :, :].rearrange("p a n -> p (a n)"),
                                 wsp[c][:, 0, :].bitcast(F32), ALU.subtract).then_inc(d_wl, 1)

            def tokens_lo(b, par):
                dve.wait_ge(a_xh, b + 1)
                v = x_hl[:, par, 1, :, :, :]
                ve.tensor_tensor(v, v.bitcast(F32), x_hl[:, par, 0, :, :, :].bitcast(F32), ALU.subtract).then_inc(d_xl, 1)

            def tile(t, i, par):
                k = 2 * t
                inverse(k + 1, 1, 0)
                maxima(k + 1, 1, 1)
                if there(t - 1):
                    rows_out(t - 1, i - 1 + par, 1 - par)
                probs_lo(k, 0)
                if there(t - 1):
                    dve.wait_ge(d_x2, t)
                    moments(1, t - 1, x2b[1 - par][:, :])
                probs_lo(k, 1)
                inverse(k + 1, 1, 1)
                if there(t - 1):
                    aggregate(1, t - 1)
                if there(t + 1):
                    maxima(k + 2, 0, 0)
                if there(t - 1):
                    variance(1, t - 1)
                probs_lo(k, 2)
                if there(t + 2):
                    first_norm(t + 2, i + 1, par)
                probs_lo(k, 3)
                if not there(t + 1):
                    tokens_lo(0, 0)
                if there(t + 2):
                    aggregate(0, t + 2)
                k = 2 * t + 1
                if there(t + 1):
                    inverse(k + 1, 0, 0)
                if there(t + 2):
                    variance(0, t + 2)
                if there(t + 1):
                    maxima(k + 1, 0, 1)
                probs_lo(k, 0)
                probs_lo(k, 1)
                if there(t + 1):
                    inverse(k + 1, 0, 1)
                    maxima(k + 2, 1, 0)
                probs_lo(k, 2)
                if not there(t + 1):
                    weights_lo(0)
                if there(t + 1):
                    values_lo(t + 1, 1 - par)
                probs_lo(k, 3)
                if not there(t + 1):
                    weights_lo(1)
            over_tiles(dve, tile)
            rows_out(NT - 1, NI - 1, 1)
            dve.wait_ge(d_x2, NT)
            moments(1, NT - 1, x2b[1][:, :])
            aggregate(1, NT - 1)
            variance(1, NT - 1)

            def hidden(b, c):
                n = SC * b + c
                p = c % 2
                dve.wait_ge(a_sg, n + 1)
                dve.wait_ge(e_u, n + 1)
                ve.tensor_tensor(sg[p][:, :], bU[p][:, :], sg[p][:, :], ALU.mult).then_inc(d_hm, 1)
                dve.wait_ge(a_hh, n + 1)
                ve.tensor_tensor(hl[p][:, :], sg[p][:, :], hh[p][:, :].bitcast(F32), ALU.subtract).then_inc(d_hl, 1)

            def outputs(b):
                dve.wait_ge(e_d, SC * (b + 1))
                for tt in range(TB):
                    n = TB * b + tt
                    dve.wait_ge(ld_xr[tt], 16 * (b + 1))
                    ve.scalar_tensor_tensor(xr[tt][:, :], bY[tt][:, :], sig[:, n:n + 1], xr[tt][:, :],
                                            ALU.mult, ALU.add).then_inc(d_out, 1)

            done = [0]

            def step_r(ins, wait=True):
                done[0] += 1
                ins.then_inc(d_r, 1)
                if wait:
                    dve.wait_ge(d_r, done[0])

            def bc(ap, shape):
                return ap.to_broadcast(shape)

            full = [P, NT, E]
            def less_maximum():
                dve.wait_ge(a_lg, NT)
                lgv = lg_all[:, :, 0:E]
                step_r(ve.tensor_reduce(nm[:, :], lgv, AX_X, ALU.max, negate=True))
                step_r(ve.tensor_tensor(ls[:, :, :], lgv, bc(nm[:, :].unsqueeze(2), full), ALU.add))
                assert done[0] == R_LS

            def probabilities():
                step_r(ve.tensor_copy(io8[:, :], io8i[:, :]))
                step_r(ve.tensor_copy(thr[:, :], thri[:, :]))
                step_r(ve.tensor_copy(sio[:, :], sioi[:, :]))
                dve.wait_ge(a_r, 2)
                step_r(ve.tensor_reduce(sm[:, :], ls[:, :, :], AX_X, ALU.add))
                step_r(ve.reciprocal(rc[:, :], sm[:, :]))
                step_r(ve.tensor_tensor(ls[:, :, :], ls[:, :, :], bc(rc[:, :].unsqueeze(2), full), ALU.mult))
                step_r(ve.tensor_scalar(ez[:, :], ez[:, :], 1.0, None, ALU.add))
                step_r(ve.reciprocal(sig[:, :], ez[:, :]))

            def two_largest():
                for t in range(NT):
                    step_r(ve.max(tv[:, t, :], ls[:, t, :]), False)
                dve.wait_ge(d_r, done[0])
                for t in range(NT):
                    step_r(ve.max_index(ti[:, t, :], tv[:, t, :], ls[:, t, :]), False)

            def one_hots():
                step_r(ve.tensor_tensor(sm[:, :], tv[:, :, 0], tv[:, :, 1], ALU.add))
                step_r(ve.reciprocal(rc[:, :], sm[:, :]))
                step_r(ve.tensor_tensor(msrc[:, :, :, 1].bitcast(F32), tv[:, :, 0:2], bc(rc[:, :].unsqueeze(2), [P, NT, 2]), ALU.mult))
                step_r(ve.tensor_copy(tif[:, :, :], ti[:, :, 0:2]))
                for k, m in enumerate((m1, m2)):
                    step_r(ve.tensor_tensor(m[:, :, :], bc(tif[:, :, k:k + 1], full), bc(io8[:, :].unsqueeze(1), full), ALU.is_equal))
                step_r(ve.tensor_tensor(ls[:, :, :], m1[:, :, :], m2[:, :, :], ALU.add))
                assert done[0] == R_M, done[0]

            def counts():
                dve.wait_ge(e_r, 1)
                step_r(ve.tensor_copy(pre_s[:, :, :], bY[0][:, 0:P].rearrange("p (t e) -> p t e", e=E)), False)
                step_r(ve.tensor_copy(tot_s[:, :, :], bY[0][:, P:2 * P].rearrange("p (t e) -> p t e", e=E)))
                assert done[0] == R_EV, done[0]

            def carries():
                step_r(ve.memset(carry[:, 0, :], 0.0))
                for t in range(1, NT):
                    step_r(ve.tensor_tensor(carry[:, t, :], carry[:, t - 1, :], tot_s[:, t - 1, :], ALU.add))
                step_r(ve.tensor_tensor(cnt[:, :], carry[:, NT - 1, :], tot_s[:, NT - 1, :], ALU.add))

            def slots():
                step_r(ve.tensor_tensor(cmpc[:, :, :], bc(cnt[:, :].unsqueeze(2), [P, E, 15]), bc(thr[:, :].unsqueeze(1), [P, E, 15]), ALU.is_gt))
                step_r(ve.tensor_reduce(nsl[:, :], cmpc[:, :, :], AX_X, ALU.add))
                step_r(ve.tensor_scalar(nsl[:, :], nsl[:, :], 1.0, None, ALU.add))
                step_r(ve.memset(sst[:, 0:1], 0.0))
                for e in range(1, E):
                    step_r(ve.tensor_tensor(sst[:, e:e + 1], sst[:, e - 1:e], nsl[:, e - 1:e], ALU.add))
                n = [1, 4 * NG + 4, E - 1]
                step_r(ve.tensor_tensor(scmp[:, :, :], bc(sio[:, :].unsqueeze(2), n), bc(sst[0:1, 1:E].unsqueeze(1), n), ALU.is_ge))
                step_r(ve.tensor_reduce(sexp[:, :, :].rearrange("o g j -> o (g j)"), scmp[:, :, :], AX_X, ALU.add))
                step_r(ve.tensor_scalar(packed[:, :], sexp[:, 1:NG + 1, 1], 1.0, None, ALU.mult))
                for at in (sexp[:, 1:NG + 1, 0], sexp[:, 0:NG, 3], sexp[:, 0:NG, 2], sexp[:, 0:NG, 1]):
                    step_r(ve.scalar_tensor_tensor(packed[:, :], packed[:, :], float(E), at, ALU.mult, ALU.add))
                step_r(ve.tensor_copy(slot_tab[:, :], packed[:, :]))
                assert done[0] == R_TAB, done[0]

            def rows():
                step_r(ve.tensor_scalar(sst[:, :], sst[:, :], float(P), None, ALU.mult))
                step_r(ve.tensor_tensor(pre_s[:, :, :], pre_s[:, :, :], carry[:, :, :], ALU.add))
                step_r(ve.tensor_tensor(pre_s[:, :, :], pre_s[:, :, :], bc(sst[:, :].unsqueeze(1), full), ALU.add))
                for k, m in enumerate((m1, m2)):
                    step_r(ve.tensor_tensor(m[:, :, :], m[:, :, :], pre_s[:, :, :], ALU.mult))
                    step_r(ve.tensor_reduce(posf[:, :, k], m[:, :, :], AX_X, ALU.add))
                step_r(ve.tensor_copy(posi[:, :, :], posf[:, :, :]))
                assert done[0] == R_POS, done[0]

            beside = {(0, 0): less_maximum, (0, 2): probabilities, (0, 3): two_largest, (0, 4): one_hots,
                      (1, 1): carries, (1, 2): slots, (1, 3): rows}

            def gate_lo(s, e):
                dve.wait_ge(a_wg, s + 1)
                ve.tensor_tensor(wg3[:, 1, :], wex[:, e, 0:W3], wg3[:, 0, :].bitcast(F32), ALU.subtract).then_inc(d_wg, 1)

            for b in range(NB):
                for c in range(SC):
                    if b == 1 and c == 1:
                        counts()
                    hidden(b, c)
                    if b == NB - 1 and c == SC - 3:
                        gate_lo(0, 0)
                    if b == 0 and c + 2 < SC:
                        weights_lo(c + 2)
                    if c == 5 and b + 1 < NB:
                        tokens_lo(b + 1, (b + 1) % 2)
                    if c == 0 and b > 0:
                        outputs(b - 1)
                    if (b, c) in beside:
                        beside[b, c]()
            def rows_lo(s, j):
                dve.wait_ge(a_xt, s + 1)
                ve.tensor_tensor(xT3[j % 2][:, 1, :, :], bX3[:, :].rearrange("p (c t) -> p c t", c=HC),
                                 xT3[j % 2][:, 0, :, :].bitcast(F32), ALU.subtract).then_inc(d_xt, 1)

            def hidden3(s, j):
                dve.wait_ge(a_sl, s + 1)
                dve.wait_ge(e_u3, s + 1)
                ve.tensor_tensor(h3[j % 2][:, 0:I], bU3[j % 2][:, 0:I], h3[j % 2][:, 0:I], ALU.mult).then_inc(d_h, 1)

            def hidden_T_lo(s, j):
                dve.wait_ge(a_ht, s + 1)
                ve.tensor_tensor(hT3[j % 2][:, 1, :, :], bH3[:, 0:IC * P].rearrange("p (c t) -> p c t", c=IC),
                                 hT3[j % 2][:, 0, :, :].bitcast(F32), ALU.subtract).then_inc(d_ht, 1)

            def up_lo(s, e):
                dve.wait_ge(a_wu, s + 1)
                ve.tensor_tensor(wu3[:, 1, :], wex[:, e, W3:2 * W3], wu3[:, 0, :].bitcast(F32), ALU.subtract).then_inc(d_wu, 1)

            def down_lo(s, e):
                dve.wait_ge(a_wd, s + 1)
                ve.tensor_tensor(wd3[:, 1, 0:2 * H], wex[:, e, 2 * W3:2 * W3 + 2 * H],
                                 wd3[:, 0, 0:2 * H].bitcast(F32), ALU.subtract).then_inc(d_wd, 1)

            rows_lo(0, 0)
            up_lo(0, 0)
            e1 = experts_from(dve, 0)[0]
            outputs(NB - 1)
            for j in range(2):
                ve.memset(h3[j][:, I:IC * P], 0.0).then_inc(d_hz, 1)
            rows_lo(1, 1)
            hidden3(0, 0)
            gate_lo(1, e1)
            up_lo(1, e1)
            down_lo(0, 0)

            def slot(s, i, j, e1, e2):
                hidden_T_lo(s, j)
                if not last_slots(s, 2):
                    rows_lo(s + 2, j + 2)
                    gate_lo(s + 2, e2)
                if not last_slots(s, 1):
                    hidden3(s + 1, j + 1)
                if not last_slots(s, 2):
                    up_lo(s + 2, e2)
                if not last_slots(s, 1):
                    down_lo(s + 1, e1)
            over_slots(dve, slot, reads_experts=True)

        @block.tensor
        def _(pe):
            te = nc.tensor

            def scores(k, t, par, s, pair):
                if pair == 0:
                    pe.wait_ge(ql_done, k + 1)
                    pe.wait_ge(kl_done, t + 1)
                after(pe, a_exp, 4 * k - 4 + 2 * pair + 2)
                for q in (2 * pair, 2 * pair + 1):
                    te.matmul(bS[q][:, :], qs[s][:, q * P:(q + 1) * P], kh[par][:, s, :], start=True, stop=False)
                    te.matmul(bS[q][:, :], qs[s][:, q * P:(q + 1) * P], kl[par][:, s, :], start=False, stop=True).then_inc(e_s, 1)

            def probs_T(k, s, c):
                if c == 0:
                    pe.wait_ge(g_pn, 4 * k + 4)
                after(pe, d_ptl, 4 * k + c - 1)
                for q in range(QC):
                    ins = te.transpose(bT[c % 2][:, q * P:(q + 1) * P], pb[s][:, q, c * P:(c + 1) * P], ident[:, :])
                ins.then_inc(e_t, 1)

            def times_v(k, t, s, par, c):
                if c == 0 and s == 0:
                    if isinstance(t, int) and t == 0:
                        pe.wait_ge(d_rg, 1)
                    pe.wait_ge(d_vl, t + 1)
                    after(pe, d_x2, t)
                hi, lo = (vs[par][:, a, c, s:s + 2, :].rearrange("p a d -> p (a d)") for a in range(2))
                first, last = s == 0 and c == 0, s == 1 and c == LC - 1
                pe.wait_ge(a_pth, 4 * k + c + 1)
                te.matmul(bO[:, :], hi, pth[c][:, :], start=first, stop=False)
                te.matmul(bO[:, :], lo, pth[c][:, :], start=False, stop=False)
                pe.wait_ge(d_ptl, 4 * k + c + 1)
                te.matmul(bO[:, :], hi, ptl[c][:, :], start=False, stop=last).then_inc(e_pv, 1)

            def values_T(t, half, par):
                pe.wait_ge(ld_cn[par], 16 * (half + 1))
                if isinstance(t, int) and t == 2:
                    pe.wait_ge(d_vl, 2)
                after(pe, a_lg, t - 2)
                for c in range(LC):
                    ins = te.transpose(bM[:, c * P:(c + 1) * P], cn[par][:, c * P:(c + 1) * P], ident[:, :])
                ins.then_inc(e_vt, 1)

            def rows_T(t, par):
                pe.wait_ge(a_x2n, t + 1)
                if isinstance(t, int) and t + 2 >= NT:
                    pe.wait_ge(a_lg, t)
                else:
                    pe.wait_ge(d_vl, t + 3)
                for c in range(HC):
                    ins = te.transpose(bM[:, c * P:(c + 1) * P], x2n[par][:, c * P:(c + 1) * P], ident[:, :])
                ins.then_inc(e_x2T, 1)

            def logits(t, par):
                pe.wait_ge(a_x2T, t + 1)
                for c in range(HC):
                    ins = te.matmul(bM[:, 0:NR], x2T[par][:, c, :], rgT[:, c, :], start=(c == 0), stop=(c == HC - 1))
                ins.then_inc(e_lg, 1)

            pe.wait_ge(g_const, N_CONST)
            values_T(0, 0, 0)
            scores(0, 0, 0, 0, 0)
            scores(0, 0, 0, 0, 1)
            scores(1, 0, 0, 1, 0)
            pe.wait_ge(ld_small, 48)
            for c in range(HC):
                ins = te.transpose(bO[:, c * NR:(c + 1) * NR], rg[:, c * P:(c + 1) * P], ident[0:NR, 0:NR])
            ins.then_inc(e_rg, 1)
            scores(1, 0, 0, 1, 1)

            def tile(t, i, par):
                k = 2 * t
                probs_T(k, 0, 0)
                probs_T(k, 0, 1)
                if there(t + 1):
                    scores(k + 2, t + 1, 1 - par, 0, 0)
                times_v(k, t, 0, par, 0)
                probs_T(k, 0, 2)
                times_v(k, t, 0, par, 1)
                probs_T(k, 0, 3)
                if there(t + 1):
                    scores(k + 2, t + 1, 1 - par, 0, 1)
                if there(t - 2):
                    logits(t - 2, par)
                times_v(k, t, 0, par, 2)
                times_v(k, t, 0, par, 3)
                k = 2 * t + 1
                probs_T(k, 1, 0)
                probs_T(k, 1, 1)
                if there(t + 1):
                    scores(k + 2, t + 1, 1 - par, 1, 0)
                times_v(k, t, 1, par, 0)
                if there(t + 1):
                    values_T(t + 1, i + par, 1 - par)
                probs_T(k, 1, 2)
                times_v(k, t, 1, par, 1)
                probs_T(k, 1, 3)
                if there(t + 1):
                    scores(k + 2, t + 1, 1 - par, 1, 1)
                times_v(k, t, 1, par, 2)
                if there(t - 1):
                    rows_T(t - 1, 1 - par)
                times_v(k, t, 1, par, 3)
            over_tiles(pe, tile)

            def gate_up(b, c, par):
                n = SC * b + c
                p = c % 2
                prev = n if c == 0 else n - 1
                if c == 0:
                    pe.wait_ge(d_xl, b + 1)
                if isinstance(b, int) and b == 0:
                    pe.wait_ge(d_wl, c + 1)
                w = wsp[c]
                for name, (bk, used, s_out) in enumerate(((bG[p], a_sg, e_g), (bU[p], d_hm, e_u))):
                    after(pe, used, prev)
                    for h in range(HC):
                        hi = w[:, 0, name * 512 + h * P:name * 512 + (h + 1) * P]
                        lo = w[:, 1, name * 512 + h * P:name * 512 + (h + 1) * P]
                        xhi, xlo = x_hl[:, par, 0, :, h, :], x_hl[:, par, 1, :, h, :]
                        te.matmul(bk[:, :], hi, xhi, start=(h == 0), stop=False)
                        te.matmul(bk[:, :], hi, xlo, start=False, stop=False)
                        ins = te.matmul(bk[:, :], lo, xhi, start=False, stop=(h == HC - 1))
                    ins.then_inc(s_out, 1)

            def down(b, c):
                n = SC * b + c
                p = c % 2
                pe.wait_ge(d_hl, n + 1)
                hi, lo = wsp[c][:, 0, 1024:1536], wsp[c][:, 1, 1024:1536]
                for tt in range(TB):
                    if c == 0:
                        after(pe, d_out, TB * b - TB + tt + 1)
                    th, tl = hh[p][:, tt * P:(tt + 1) * P], hl[p][:, tt * P:(tt + 1) * P]
                    te.matmul(bY[tt][:, :], th, hi, start=(c == 0), stop=False)
                    te.matmul(bY[tt][:, :], th, lo, start=False, stop=False)
                    ins = te.matmul(bY[tt][:, :], tl, hi, start=False, stop=(c == SC - 1))
                ins.then_inc(e_d, 1)

            def rows3(s, half, j):
                pe.wait_ge(ld_xg[j % 2], 16 * (half + 1))
                after(pe, d_xt, s)
                for c in range(HC):
                    ins = te.transpose(bX3[:, c * P:(c + 1) * P], xg[j % 2][:, c * P:(c + 1) * P], ident[:, :])
                ins.then_inc(e_tx, 1)

            def block2(b, par, last):
                for c in range(1, SC):
                    gate_up(b, c, par)
                    if b == 0 and c == 1:
                        pe.wait_ge(a_lg, NT)
                        pe.wait_ge(d_x2, NT)
                    if b == 1 and c == 1:
                        pe.wait_ge(d_r, R_M)
                        pe.wait_ge(d_out, 1)
                        te.matmul(bY[0][:, 0:P], tri[:, :], ls[:, :, :].rearrange("p t e -> p (t e)"), start=True, stop=True)
                        te.matmul(bY[0][:, P:2 * P], ones[:, :], ls[:, :, :].rearrange("p t e -> p (t e)"), start=True, stop=True).then_inc(e_r, 1)
                        pe.wait_ge(d_r, R_EV)
                    down(b, c - 1)
                if not last:
                    gate_up(b + 1, 0, 1 - par)
                else:
                    rows3(0, 0, 0)
                down(b, SC - 1)
                if last:
                    rows3(1, 0, 1)

            logits(NT - 2, 0)
            gate_up(0, 0, 0)
            rows_T(NT - 1, 1)
            logits(NT - 1, 1)
            for b in range(NB):
                block2(b, b % 2, b == NB - 1)

            def gate_or_up(s, j, m):
                bk, w, ready, used, done3 = ((bG3[j % 2], wg3, d_wg, a_sl, e_g3), (bU3[j % 2], wu3, d_wu, d_h, e_u3))[m]
                if m == 0:
                    pe.wait_ge(d_xt, s + 1)
                pe.wait_ge(ready, s + 1)
                after(pe, used, s - 1)
                for c in range(HC):
                    hi, lo = (w[:, a, c * I:(c + 1) * I] for a in range(2))
                    xhi, xlo = xT3[j % 2][:, 0, c, :], xT3[j % 2][:, 1, c, :]
                    te.matmul(bk[:, 0:I], xhi, hi, start=(c == 0), stop=False)
                    te.matmul(bk[:, 0:I], xhi, lo, start=False, stop=False)
                    ins = te.matmul(bk[:, 0:I], xlo, hi, start=False, stop=(c == HC - 1))
                ins.then_inc(done3, 1)

            def hidden_T(s, j):
                if isinstance(s, int) and s == 0:
                    pe.wait_ge(d_hz, 2)
                pe.wait_ge(d_h, s + 1)
                after(pe, d_ht, s)
                for c in range(IC):
                    ins = te.transpose(bH3[:, c * P:(c + 1) * P], h3[j % 2][:, c * P:(c + 1) * P], ident[:, :])
                ins.then_inc(e_th, 1)

            def down3(s, j):
                pe.wait_ge(d_ht, s + 1)
                pe.wait_ge(d_wd, s + 1)
                after(pe, a_y, s - 1)
                for c in range(IC):
                    n = P if c < IC - 1 else IR
                    if c == IC - 1:
                        pe.wait_ge(g_wd, s + 1)
                    hi, lo = (wd3[0:n, a, c * H:(c + 1) * H] for a in range(2))
                    thi, tlo = hT3[j % 2][0:n, 0, c, :], hT3[j % 2][0:n, 1, c, :]
                    te.matmul(bY3[j % 2][:, :], thi, hi, start=(c == 0), stop=False)
                    te.matmul(bY3[j % 2][:, :], thi, lo, start=False, stop=False)
                    ins = te.matmul(bY3[j % 2][:, :], tlo, hi, start=False, stop=(c == IC - 1))
                ins.then_inc(e_d3, 1)

            gate_or_up(0, 0, 0)
            gate_or_up(0, 0, 1)
            pe.wait_ge(d_out, NT)

            def slot(s, i, j, e1, e2):
                if not last_slots(s, 2):
                    rows3(s + 2, 2 * i + (j + 2) // 2, j + 2)
                if not last_slots(s, 1):
                    gate_or_up(s + 1, j + 1, 0)
                hidden_T(s, j)
                if not last_slots(s, 1):
                    gate_or_up(s + 1, j + 1, 1)
                down3(s, j)
            over_slots(pe, slot)


def kernel(**inputs):
    import numpy as np
    import concourse.bacc as bacc
    from concourse.bass_utils import run_bass_kernel_spmd

    names = ["x", "ctx_2048", "L0_xattn_gamma", "L0_ffn_router_w", "L0_ffn_w_gate", "L0_ffn_w_up", "L0_ffn_w_down",
             "L0_ffn_sw_gate", "L0_ffn_sw_up", "L0_ffn_sw_down", "L0_ffn_shared_gate_w"]
    nc = bacc.Bacc("TRN2", target_bir_lowering=False, num_devices=1)
    arrays, args = {}, []
    for name in names:
        a = np.ascontiguousarray(inputs[name])
        if a.ndim == 0:
            a = a.reshape(1)
        arrays[f"in_{name}"] = a
        args.append(nc.dram_tensor(f"in_{name}", a.shape, mybir.dt.from_np(a.dtype), kind="ExternalInput").ap())
    shape = inputs["x"].shape
    rows = shape[0] * shape[1]
    args.append(nc.dram_tensor("out", (rows + P, shape[2]), F32, kind="ExternalOutput").ap())
    xattn_moe_kernel(nc, *args)
    r = run_bass_kernel_spmd(nc, [arrays], core_ids=[0])
    return r.results[0]["out"][:rows].reshape(shape)
```
